# Optimizing a Trainium2 kernel written in Bass

```python
import numpy as np
import jax
import jax.numpy as jnp

def _softmax(x, axis=-1):
    return jax.nn.softmax(x, axis=axis)

def _gelu(x):
    return jax.nn.gelu(x, approximate=True)

def _silu(x):
    return jax.nn.silu(x)

def _sigmoid(x):
    return jax.nn.sigmoid(x)

def _layernorm(x, axis=-1, eps=1e-05):
    m = jnp.mean(x, axis=axis, keepdims=True)
    v = jnp.var(x, axis=axis, keepdims=True)
    return (x - m) / jnp.sqrt(v + eps)

def _scatter_add(tgt, idx, src, axis=0):
    return tgt.at[idx].add(src)

def _segment_sum(src, seg, n):
    return jax.ops.segment_sum(src, seg, n)
kernel_name = 'mk_seq_postln_d1_jaxref_r8_0fd8a5'

def setup_inputs(seed: int=0):
    np.random.seed(seed)
    _w = jnp.asarray

    def _L0_attn_setup():
        import jax, jax.numpy as jnp
        import numpy as np
        D_MODEL = 128
        D_STATE = 16
        LN_EPS = 1e-05

        def _layernorm(x, w, b):
            mu = jnp.mean(x, axis=-1, keepdims=True)
            var = jnp.mean(jnp.square(x - mu), axis=-1, keepdims=True)
            return (x - mu) * jax.lax.rsqrt(var + LN_EPS) * w + b
        key = jax.random.key(seed)
        ks = jax.random.split(key, 12)
        B, S, D, N = (8, 512, D_MODEL, D_STATE)
        sD = 1.0 / np.sqrt(D)
        sN = 1.0 / np.sqrt(N)
        return {'x': jax.random.normal(ks[0], (B, S, D), dtype=jnp.float32), 'Ws': jax.random.uniform(ks[1], (N, D), jnp.float32, -sD, sD), 'bs': jax.random.uniform(ks[2], (N,), jnp.float32, -sD, sD), 'Wi': jax.random.uniform(ks[3], (N, D), jnp.float32, -sD, sD), 'bi': jax.random.uniform(ks[4], (N,), jnp.float32, -sD, sD), 'Wo': jax.random.uniform(ks[5], (D, N), jnp.float32, -sN, sN), 'bo': jax.random.uniform(ks[6], (D,), jnp.float32, -sN, sN), 'Wg': jax.random.uniform(ks[7], (D, D), jnp.float32, -sD, sD), 'bg': jax.random.uniform(ks[8], (D,), jnp.float32, -sD, sD), 'ln_w': jnp.ones((D,), jnp.float32), 'ln_b': jnp.zeros((D,), jnp.float32), 'A': jax.random.normal(ks[9], (N, N), dtype=jnp.float32) * 0.01}
    _L0_attn_in = _L0_attn_setup()

    def _L0_ffn_setup():
        import jax, jax.numpy as jnp
        import numpy as np
        from jax import lax
        D = 128
        H = 176
        E = 8
        K = 2
        ROUTER_SCALE = 1.0

        def _expert(x, w1, b1, w3, b3, w2, b2):
            h = jax.nn.silu((x @ w1 + b1) * (x @ w3 + b3))
            return h @ w2 + b2
        key = jax.random.key(seed)
        ks = jax.random.split(key, 16)
        s = 0.02
        inp = {'x': jax.random.normal(ks[0], (2, 256, D), dtype=jnp.float32), 'gate_w': jax.random.normal(ks[1], (E, D), dtype=jnp.float32) * s, 'gate_b': jax.random.normal(ks[2], (E,), dtype=jnp.float32) * s, 'w1': jax.random.normal(ks[3], (E, D, H), dtype=jnp.float32) * s, 'b1': jax.random.normal(ks[4], (E, H), dtype=jnp.float32) * s, 'w3': jax.random.normal(ks[5], (E, D, H), dtype=jnp.float32) * s, 'b3': jax.random.normal(ks[6], (E, H), dtype=jnp.float32) * s, 'w2': jax.random.normal(ks[7], (E, H, D), dtype=jnp.float32) * s, 'b2': jax.random.normal(ks[8], (E, D), dtype=jnp.float32) * s, 'sw1': jax.random.normal(ks[9], (D, H), dtype=jnp.float32) * s, 'sb1': jax.random.normal(ks[10], (H,), dtype=jnp.float32) * s, 'sw3': jax.random.normal(ks[11], (D, H), dtype=jnp.float32) * s, 'sb3': jax.random.normal(ks[12], (H,), dtype=jnp.float32) * s, 'sw2': jax.random.normal(ks[13], (H, D), dtype=jnp.float32) * s, 'sb2': jax.random.normal(ks[14], (D,), dtype=jnp.float32) * s}
        return inp
    _L0_ffn_in = _L0_ffn_setup()
    _d = {'L0_attn_x': _L0_attn_in['x'], 'L0_attn_Ws': _L0_attn_in['Ws'], 'L0_attn_bs': _L0_attn_in['bs'], 'L0_attn_Wi': _L0_attn_in['Wi'], 'L0_attn_bi': _L0_attn_in['bi'], 'L0_attn_Wo': _L0_attn_in['Wo'], 'L0_attn_bo': _L0_attn_in['bo'], 'L0_attn_Wg': _L0_attn_in['Wg'], 'L0_attn_bg': _L0_attn_in['bg'], 'L0_attn_ln_w': _L0_attn_in['ln_w'], 'L0_attn_ln_b': _L0_attn_in['ln_b'], 'L0_attn_A': _L0_attn_in['A'], 'L0_ffn_gate_w': _L0_ffn_in['gate_w'], 'L0_ffn_gate_b': _L0_ffn_in['gate_b'], 'L0_ffn_w1': _L0_ffn_in['w1'], 'L0_ffn_b1': _L0_ffn_in['b1'], 'L0_ffn_w3': _L0_ffn_in['w3'], 'L0_ffn_b3': _L0_ffn_in['b3'], 'L0_ffn_w2': _L0_ffn_in['w2'], 'L0_ffn_b2': _L0_ffn_in['b2'], 'L0_ffn_sw1': _L0_ffn_in['sw1'], 'L0_ffn_sb1': _L0_ffn_in['sb1'], 'L0_ffn_sw3': _L0_ffn_in['sw3'], 'L0_ffn_sb3': _L0_ffn_in['sb3'], 'L0_ffn_sw2': _L0_ffn_in['sw2'], 'L0_ffn_sb2': _L0_ffn_in['sb2']}
    _x0 = _d['L0_attn_x']
    _d['L0_attn_x'] = jax.random.normal(jax.random.fold_in(jax.random.key(seed), 1), (32, 256, 128), dtype=_x0.dtype)
    del _x0
    return _d

def reference(L0_attn_x, L0_attn_Ws, L0_attn_bs, L0_attn_Wi, L0_attn_bi, L0_attn_Wo, L0_attn_bo, L0_attn_Wg, L0_attn_bg, L0_attn_ln_w, L0_attn_ln_b, L0_attn_A, L0_ffn_gate_w, L0_ffn_gate_b, L0_ffn_w1, L0_ffn_b1, L0_ffn_w3, L0_ffn_b3, L0_ffn_w2, L0_ffn_b2, L0_ffn_sw1, L0_ffn_sb1, L0_ffn_sw3, L0_ffn_sb3, L0_ffn_sw2, L0_ffn_sb2):

    def _L0_attn_ref(x, Ws, bs, Wi, bi, Wo, bo, Wg, bg, ln_w, ln_b, A):
        import jax, jax.numpy as jnp
        import numpy as np
        D_MODEL = 128
        D_STATE = 16
        LN_EPS = 1e-05

        def _layernorm(x, w, b):
            mu = jnp.mean(x, axis=-1, keepdims=True)
            var = jnp.mean(jnp.square(x - mu), axis=-1, keepdims=True)
            return (x - mu) * jax.lax.rsqrt(var + LN_EPS) * w + b
        B, S, D = x.shape
        residual = x
        xn = _layernorm(x, ln_w, ln_b)
        u = jnp.einsum('bsd,nd->bsn', xn, Ws) + bs + jnp.einsum('bsd,nd->bsn', xn, Wi) + bi
        h0 = jnp.zeros((B, A.shape[0]), x.dtype)

        def step(h, u_t):
            h = jnp.tanh(h @ A.T + u_t)
            return (h, h)
        _, H = jax.lax.scan(step, h0, jnp.swapaxes(u, 0, 1))
        H = jnp.swapaxes(H, 0, 1)
        out = jnp.einsum('bsn,dn->bsd', H, Wo) + bo
        gate = jax.nn.sigmoid(jnp.einsum('bsd,ed->bse', xn, Wg) + bg)
        return out * gate + residual

    def _L0_ffn_ref(x, gate_w, gate_b, w1, b1, w3, b3, w2, b2, sw1, sb1, sw3, sb3, sw2, sb2):
        import jax, jax.numpy as jnp
        import numpy as np
        from jax import lax
        D = 128
        H = 176
        E = 8
        K = 2
        ROUTER_SCALE = 1.0

        def _expert(x, w1, b1, w3, b3, w2, b2):
            h = jax.nn.silu((x @ w1 + b1) * (x @ w3 + b3))
            return h @ w2 + b2
        shape = x.shape
        xf = x.reshape(-1, D)
        T = xf.shape[0]
        scores = jax.nn.softmax(xf @ gate_w.T, axis=-1)
        biased = scores + gate_b
        _, idx = lax.top_k(biased, K)
        w = jnp.take_along_axis(scores, idx, axis=-1) * ROUTER_SCALE
        rw = jnp.zeros((T, E), dtype=xf.dtype).at[jnp.arange(T)[:, None], idx].add(w)
        h = jax.nn.silu((jnp.einsum('td,edh->teh', xf, w1) + b1) * (jnp.einsum('td,edh->teh', xf, w3) + b3))
        oe = jnp.einsum('teh,ehd->ted', h, w2) + b2
        y = jnp.einsum('te,ted->td', rw, oe)
        z = _expert(xf, sw1, sb1, sw3, sb3, sw2, sb2)
        return (y + z).reshape(shape)
    x = L0_attn_x
    x = _layernorm(x + _L0_attn_ref(x, L0_attn_Ws, L0_attn_bs, L0_attn_Wi, L0_attn_bi, L0_attn_Wo, L0_attn_bo, L0_attn_Wg, L0_attn_bg, L0_attn_ln_w, L0_attn_ln_b, L0_attn_A), axis=-1)
    x = _layernorm(x + _L0_ffn_ref(x, L0_ffn_gate_w, L0_ffn_gate_b, L0_ffn_w1, L0_ffn_b1, L0_ffn_w3, L0_ffn_b3, L0_ffn_w2, L0_ffn_b2, L0_ffn_sw1, L0_ffn_sb1, L0_ffn_sw3, L0_ffn_sb3, L0_ffn_sw2, L0_ffn_sb2), axis=-1)
    return x

_drawn_inputs = setup_inputs


def setup_inputs(seed=0):
    import zlib

    import numpy as np

    out = dict(_drawn_inputs(seed))
    spreads = {'L0_attn_ln_w': (1.0, 0.6), 'L0_attn_ln_b': (0.0, 0.8)}
    factors = {'L0_attn_bs': 8.0,
     'L0_attn_bi': 8.0,
     'L0_attn_bg': 8.0,
     'L0_attn_A': 8.0,
     'L0_ffn_gate_w': 8.0,
     'L0_ffn_gate_b': 8.0,
     'L0_ffn_w1': 8.0,
     'L0_ffn_b1': 8.0,
     'L0_ffn_w3': 8.0,
     'L0_ffn_b3': 8.0,
     'L0_ffn_w2': 8.0,
     'L0_ffn_b2': 29.019,
     'L0_ffn_sw1': 8.0,
     'L0_ffn_sb1': 8.0,
     'L0_ffn_sw3': 8.0,
     'L0_ffn_sb3': 8.0,
     'L0_ffn_sw2': 8.0,
     'L0_ffn_sb2': 15.887}
    for name, (base, spread) in spreads.items():
        noise = np.random.default_rng([zlib.crc32(name.encode()), seed]).standard_normal(out[name].shape)
        drawn = base * np.exp(spread * noise) if base else spread * noise
        out[name] = jnp.asarray(drawn.astype(out[name].dtype))
    for name, factor in factors.items():
        out[name] = (out[name] * factor).astype(out[name].dtype)
    return out
```

```python
import concourse.bass as bass
from concourse import mybir
from contextlib import ExitStack


def rnn_gate_moe_block(nc, x, Ws, bs, Wi, bi, Wo, bo, Wg, bg, ln_w, ln_b, A,
                       gate_w, gate_b, w1, b1, w3, b3, w2, b2, sw1, sb1, sw3, sb3, sw2, sb2, out):
    fp32, fp32r = mybir.dt.float32, mybir.dt.float32r
    ALU, ACT, AX = mybir.AluOpType, mybir.ActivationFunctionType, mybir.AxisListType

    B, S, D = x.shape
    N = A.shape[0]
    E, _, H = w1.shape
    P = 128
    STEPS = 16
    TOK = B * STEPS
    Q = TOK // P
    TILES = S // STEPS
    CH = E * H // P
    REST = H - P
    POS = CH + 2
    HID = (CH + 1) * P
    M13 = 64 + REST
    EPS = 1e-5
    SOFT = 18
    NAPIER = 2.718281828459045

    xv = x.rearrange("b (k tq q) d -> k b tq (q d)", tq=STEPS // Q, q=Q)
    ov = out.rearrange("b (k tq q) d -> k b tq (q d)", tq=STEPS // Q, q=Q)

    with ExitStack() as ctx:
        def sb(name, shape, dt=fp32):
            return ctx.enter_context(nc.sbuf_tensor(name, shape, dt))

        def pb(name, shape=(P, TOK)):
            return ctx.enter_context(nc.psum_tensor(name, list(shape), fp32))

        def sem(name):
            return ctx.enter_context(nc.semaphore(name))

        ident = sb("ident", [P, P])
        neghalf = sb("neghalf", [P, Q])
        scratch = sb("scratch", [P, 1])
        eps1, eps4 = sb("eps1", [P, Q]), sb("eps4", [P, Q])
        primer = sb("primer", [P, Q])
        napier = sb("napier", [P, Q, E])
        rev = sb("rev", [P, E])
        ws_t, wi_t, wsi_t = sb("ws_t", [N, D]), sb("wi_t", [N, D]), sb("wsi_t", [N, D])
        wo_t = sb("wo_t", [D, N])
        vrow, vcol = sb("vrow", [32, P]), sb("vcol", [P, 32])
        wg_t, gw_t, a_t = sb("wg_t", [D, D]), sb("gw_t", [E, D]), sb("a_t", [N, N])
        wsiT, woT, wgT, aT = sb("wsiT", [D, P]), sb("woT", [N + 1, D]), sb("wgT", [D, D]), sb("aT", [N, P])
        gwTh, gwTl = sb("gwTh", [D, E], fp32r), sb("gwTl", [D, E], fp32r)
        bu, bgh = sb("bu", [N, 1]), sb("bgh", [D, 1])
        gb = sb("gb", [P, E])
        w1f, w3f = sb("w1f", [D, HID + M13]), sb("w3f", [D, HID])
        w1h, w1l = sb("w1h", [D, HID + M13], fp32r), sb("w1l", [D, HID + M13], fp32r)
        w3h, w3l = sb("w3h", [D, HID], fp32r), sb("w3l", [D, HID], fp32r)
        b1c, b3c = vcol[:, 0:POS], vcol[:, POS:2 * POS]
        bgc, lnw, lnb = (vcol[:, 2 * POS + i:2 * POS + i + 1] for i in range(3))
        bsc, bic = vcol[0:N, 29:30], vcol[0:N, 30:31]
        w2t = sb("w2t", [P, POS, D])
        self_, sel = sb("self_", [P, CH * P]), sb("sel", [P, CH * P], fp32r)

        xt = [sb(f"xt{i}", [P, Q, D]) for i in range(2)]
        xn = sb("xn", [P, Q, D])
        xnT = sb("xnT", [D, TOK])
        gth = [sb(f"gth{i}", [D, TOK]) for i in range(2)]
        hT = sb("hT", [N + 1, TOK])
        og = sb("og", [D, TOK])
        x1 = [sb(f"x1{i}", [P, Q, D]) for i in range(2)]
        x1h = [sb(f"x1h{i}", [D, TOK], fp32r) for i in range(2)]
        x1l = [sb(f"x1l{i}", [D, TOK], fp32r) for i in range(2)]
        rwT = sb("rwT", [P, TOK], fp32r)
        rt = sb("rt", [P, Q, P])
        t3, zt = sb("t3", [P, TOK]), sb("zt", [P, TOK])
        sl = [sb(f"sl{i}", [P, TOK]) for i in range(2)]
        sh0, sh1 = sb("sh0", [P, TOK]), sb("sh1", [P, TOK])
        st = [sb(f"st{i}", [P, TOK]) for i in range(3)]
        yT = sb("yT", [D, TOK])
        yo = sb("yo", [P, Q, D])
        stats = {w: sb(f"stats_{w}", [P, Q, 6]) for w in ("in", "mid", "out")}
        mv = {w: sb(f"mv_{w}", [P, Q, 2]) for w in ("in", "mid", "out")}
        ve = {w: sb(f"ve_{w}", [P, Q]) for w in ("in", "mid", "out")}
        rstd = {w: sb(f"rstd_{w}", [P, Q]) for w in ("in", "mid", "out")}
        row = {w: sb(f"row_{w}", [P, Q]) for w in ("max", "sum", "inv", "m1", "i1", "m2", "i2")}
        ex8 = {w: sb(f"ex8_{w}", [P, Q, E]) for w in
               ("ls", "ex", "sc", "bz", "c1", "d1", "o1", "bz2", "c2", "d2", "o2", "mk", "rw")}
        rwh = sb("rwh", [P, Q, E], fp32r)

        p1 = [pb(f"p1_{i}") for i in range(2)]
        p3 = [pb(f"p3_{i}") for i in range(2)]
        prw, py, pu, pm = pb("prw"), pb("py"), pb("pu"), pb("pm")

        s_rows, rows_zeroed = sem("s_rows"), sem("rows_zeroed")
        s_small, s_big, s_w2 = sem("s_small"), sem("s_big"), sem("s_w2")
        id_made, const_made, pool_step = sem("id_made"), sem("const_made"), sem("pool_step")
        w2_zeroed, setup_tr, setup_ev, setup_dve, sel_ready = (
            sem("w2_zeroed"), sem("setup_tr"), sem("setup_ev"), sem("setup_dve"), sem("sel_ready"))
        x_loaded = [sem("x_loaded0"), sem("x_loaded1")]
        out_stored = sem("out_stored")
        bn_done = {w: sem(f"bn_done_{w}") for w in ("in", "mid", "out")}
        mv_ready = {w: sem(f"mv_ready_{w}") for w in ("in", "mid", "out")}
        pool_r = {w: sem(f"pool_r_{w}") for w in ("in", "mid", "out")}
        xn_ready, xnT_ps, xnT_ready = sem("xn_ready"), sem("xnT_ps"), sem("xnT_ready")
        gate_ps, gate_ready = sem("gate_ps"), sem("gate_ready")
        h_ps, h_ready = sem("h_ps"), sem("h_ready")
        ho_ps, og_ready, ogT_ps, v_ready = sem("ho_ps"), sem("og_ready"), sem("ogT_ps"), sem("v_ready")
        x1_ready, x1T_ps, x1h_ready, x1l_ready = sem("x1_ready"), sem("x1T_ps"), sem("x1h_ready"), sem("x1l_ready")
        lg_ps, ls_ready, ex_ready, soft_step = sem("lg_ps"), sem("ls_ready"), sem("ex_ready"), sem("soft_step")
        rt_ready, rwT_ps, rwT_ready = sem("rt_ready"), sem("rwT_ps"), sem("rwT_ready")
        up_ps, t3_ready, z_ready, sl_ready = sem("up_ps"), sem("t3_ready"), sem("z_ready"), sem("sl_ready")
        rwb_ps, s_ready, down_ps = sem("rwb_ps"), sem("s_ready"), sem("down_ps")
        yT_ready, y_ps, v2_ready, yo_ready = sem("yT_ready"), sem("y_ps"), sem("v2_ready"), sem("yo_ready")

        block = ctx.enter_context(nc.Block())

        def wait(eng, s, v):
            if not (isinstance(v, int) and v <= 0):
                eng.wait_ge(s, v)

        def iterations(eng, one):
            def straight(k):
                one(k, k % 2, k // 2, 0 <= k < TILES, 0 <= k + 1 < TILES, k + 2 < TILES, 0 <= k - 1)
            for k in (-2, -1, 0):
                straight(k)
            with eng.Fori(0, (TILES - 4) // 2) as j:
                one(2 * j + 1, 1, j, True, True, True, True)
                one(2 * j + 2, 0, j + 1, True, True, True, True)
            for k in range(TILES - 3, TILES + 1):
                straight(k)

        def cols(pos):
            if pos == 0:
                return slice(CH * P, HID)
            if pos == 1:
                return slice(HID, HID + M13)
            return slice((pos - 2) * P, (pos - 1) * P)

        def s_tile(pos):
            return sh0 if pos == 0 else sh1 if pos == 1 else st[pos % 3]

        def step_cols(t):
            tq, q = divmod(t, Q)
            return slice(q * P + tq, (q + 1) * P, STEPS // Q)

        @block.sync
        def _(sp):
            for dst, src in ((ws_t, Ws), (wi_t, Wi), (a_t, A), (gw_t, gate_w), (wg_t, Wg), (wo_t, Wo)):
                sp.dma_start(dst[:, :], src).then_inc(s_small, 16)
            sp.dma_start(xt[0][:, :, :].rearrange("p q d -> p (q d)"), xv[0]).then_inc(x_loaded[0], 16)
            sp.dma_start(woT[N:N + 1, :], bo.rearrange("(a d) -> a d", a=1)).then_inc(s_small, 16)
            sp.dma_start(gb[:, :], gate_b.partition_broadcast(P)).then_inc(s_small, 16)
            sp.dma_start(xt[1][:, :, :].rearrange("p q d -> p (q d)"), xv[1]).then_inc(x_loaded[1], 16)
            sp.dma_start(w2t[:, 2:POS, :], w2.rearrange("e h d -> (e h) d").rearrange("(c p) d -> p c d", p=P)).then_inc(s_w2, 16)
            sp.dma_start(w2t[:, 0, :], sw2[0:P, :]).then_inc(s_w2, 16)
            sp.wait_ge(w2_zeroed, 1)
            sp.dma_start(w2t[0:REST, 1, :], sw2[P:H, :]).then_inc(s_w2, 16)
            for at in (64, 96):
                sp.dma_start(w2t[at:at + E, 1, :], b2).then_inc(s_w2, 16)
                sp.dma_start(w2t[at + E:at + E + 1, 1, :], sb2.rearrange("(a d) -> a d", a=1)).then_inc(s_w2, 16)

            def one(k, par, half, moe, attn, norm, fin):
                if fin:
                    sp.wait_ge(yo_ready, k)
                    sp.dma_start(ov[bass.ds(k - 1, 1)].rearrange("a b t f -> (a b) t f") if not isinstance(k, int) else ov[k - 1],
                                 yo[:, :, :].rearrange("p q d -> p (q d)")).then_inc(out_stored, 16)
                if attn and (not isinstance(k, int) or k + 3 < TILES):
                    sp.wait_ge(v_ready, k + 2)
                    sp.dma_start(xt[1 - par][:, :, :].rearrange("p q d -> p (q d)"),
                                 xv[bass.ds(k + 3, 1)].rearrange("a b t f -> (a b) t f") if not isinstance(k, int) else xv[k + 3]
                                 ).then_inc(x_loaded[1 - par], 16)
            iterations(sp, one)
            sp.wait_ge(out_stored, 16 * TILES)

        @block.gpsimd
        def _(g):
            g.memset(ident[:, :], 0.0).then_inc(pool_step, 1)
            g.wait_ge(pool_step, 1)
            g.affine_select(out=ident[:, :], in_=ident[:, :], compare_op=ALU.not_equal, fill=1.0,
                            base=0, pattern=[[-1, P]], channel_multiplier=1).then_inc(id_made, 1)
            g.memset(neghalf[:, :], -0.5)
            g.memset(eps1[:, :], EPS)
            g.memset(eps4[:, :], 4 * EPS)
            g.memset(napier[:, :, :], NAPIER)
            for j in range(E):
                g.memset(rev[:, j:j + 1], float(E - j))
            g.memset(rt[:, :, :], 0.0).then_inc(pool_step, 1)
            g.wait_ge(pool_step, 2)
            g.memset(rt[:, :, E:E + 1], 1.0)
            g.memset(rt[:, :, 64 + E:65 + E], 1.0).then_inc(const_made, 1)
            g.wait_ge(const_made, 1)
            g.wait_ge(sel_ready, 1)
            n = 2
            for r in (0, 32):
                v = self_[r:r + 32, :]
                g.affine_select(out=v, in_=v, compare_op=ALU.is_ge, fill=0.0,
                                base=0, pattern=[[1, CH * P]], channel_multiplier=-H).then_inc(pool_step, 1)
                n += 1
                g.wait_ge(pool_step, n)
                g.affine_select(out=v, in_=v, compare_op=ALU.is_ge, fill=0.0,
                                base=H - 1, pattern=[[-1, CH * P]], channel_multiplier=H).then_inc(pool_step, 1)
                n += 1
                g.wait_ge(pool_step, n)

            def rsqrt(w, tile, eps_t):
                g.wait_ge(mv_ready[w], tile + 1)
                g.tensor_tensor(out=ve[w][:, :], in0=mv[w][:, :, 1], in1=eps_t[:, :], op=ALU.add).then_inc(pool_r[w], 1)
                g.wait_ge(pool_r[w], 2 * tile + 1)
                g.tensor_tensor(out=rstd[w][:, :], in0=ve[w][:, :], in1=neghalf[:, :], op=ALU.pow).then_inc(pool_r[w], 1)

            def one(k, par, half, moe, attn, norm, fin):
                if norm:
                    rsqrt("in", k + 2, eps1)
                if fin:
                    rsqrt("out", k - 1, eps1)
                if attn:
                    rsqrt("mid", k + 1, eps4)
                    g.wait_ge(ls_ready, k + 2)
                    g.tensor_tensor(out=ex8["ex"][:, :, :], in0=napier[:, :, :], in1=ex8["ls"][:, :, :],
                                    op=ALU.pow).then_inc(ex_ready, 1)
            iterations(g, one)

        @block.scalar
        def _(act):
            act.wait_ge(rows_zeroed, 1)
            for r, at, src, ssrc in ((0, 0, b1, sb1), (POS, 64, b3, sb3)):
                act.dma_start(vrow[r + 2:r + POS, :], src.rearrange("e h -> (e h)").rearrange("(c p) -> c p", p=P)).then_inc(s_rows, 16)
                act.dma_start(vrow[r:r + 1, :], ssrc[0:P].rearrange("(a d) -> a d", a=1)).then_inc(s_rows, 16)
                act.dma_start(vrow[r + 1:r + 2, at:at + REST], ssrc[P:H].rearrange("(a d) -> a d", a=1)).then_inc(s_rows, 16)
            for r, src in enumerate((bg, ln_w, ln_b, bs, bi)):
                act.dma_start(vrow[2 * POS + r:2 * POS + r + 1, 0:src.shape[0]], src.rearrange("(a d) -> a d", a=1)).then_inc(s_rows, 16)
            act.dma_start(w1f[:, 0:CH * P].rearrange("d (e h) -> d e h", e=E), w1.rearrange("e d h -> d e h")).then_inc(s_big, 16)
            act.dma_start(w3f[:, 0:CH * P].rearrange("d (e h) -> d e h", e=E), w3.rearrange("e d h -> d e h")).then_inc(s_big, 16)
            act.dma_start(w1f[:, CH * P:HID + REST], sw1).then_inc(s_big, 16)
            act.dma_start(w3f[:, CH * P:HID], sw3[:, 0:P]).then_inc(s_big, 16)
            act.dma_start(w1f[:, HID + 64:HID + M13], sw3[:, P:H]).then_inc(s_big, 16)
            act.wait_ge(const_made, 1)
            nc.scalar.activation(primer[:, :], neghalf[:, :], ACT.Silu)

            def side(slot, k, par, half, moe, attn, norm, fin):
                if slot == 1 and moe:
                    act.wait_ge(rwT_ps, k + 1)
                    nc.scalar.activation(rwT[:, :], pm[:, :], ACT.Identity)
                    nc.scalar.activation(sh1[64:P, :], pm[64:P, :], ACT.Identity).then_inc(rwT_ready, 1)
                if attn and 2 <= slot < 2 + STEPS:
                    t = slot - 2
                    c = step_cols(t)
                    n = STEPS * (k + 1) + t
                    act.wait_ge(h_ps, n + 1)
                    nc.scalar.activation(hT[0:N, c], pu[0:N, c], ACT.Tanh, bias=bu[:, 0:1]).then_inc(h_ready, 1)
                if slot == 5 and fin:
                    act.wait_ge(down_ps, POS * k)
                    wait(act, y_ps, k - 1)
                    nc.scalar.activation(yT[:, :], py[:, :], ACT.Identity).then_inc(yT_ready, 1)
                if slot == 12 and norm:
                    act.wait_ge(xnT_ps, k + 3)
                    nc.scalar.activation(xnT[:, :], pm[:, :], ACT.Identity, scale=lnw,
                                         bias=lnb).then_inc(xnT_ready, 1)
                if slot == 15 and norm:
                    act.wait_ge(gate_ps, k + 3)
                    wait(act, og_ready, k + 1)
                    nc.scalar.activation(gth[par][:, :], pm[:, :], ACT.Tanh, scale=0.5,
                                         bias=bgh[:, 0:1]).then_inc(gate_ready, 1)
                if slot == 29 and attn:
                    act.wait_ge(x1T_ps, k + 2)
                    nc.scalar.activation(x1h[1 - par][:, :], pm[:, :], ACT.Identity).then_inc(x1h_ready, 1)

            def silu(pos, k):
                act.wait_ge(z_ready, POS * k + pos + 1)
                if pos == 0:
                    wait(act, down_ps, POS * (k - 1) + 1)
                    nc.scalar.activation(sh0[:, :], zt[:, :], ACT.Silu).then_inc(sl_ready, 1)
                elif pos == 1:
                    wait(act, down_ps, POS * (k - 1) + 2)
                    nc.scalar.activation(sh1[0:REST, :], zt[0:REST, :], ACT.Silu).then_inc(sl_ready, 1)
                else:
                    wait(act, s_ready, CH * k + max(pos - 3, 0))
                    nc.scalar.activation(sl[pos % 2][:, :], zt[:, :], ACT.Silu).then_inc(sl_ready, 1)

            def one(k, par, half, moe, attn, norm, fin):
                for pos in range(POS):
                    if moe and pos >= 1:
                        silu(pos - 1, k)
                    elif fin and pos == 0:
                        silu(POS - 1, k - 1)
                    side(3 * pos, k, par, half, moe, attn, norm, fin)
                    if moe:
                        act.wait_ge(up_ps, POS * k + pos + 1)
                        if pos == 1:
                            nc.scalar.activation(t3[0:REST, :], p1[par ^ 1][64:M13, :], ACT.Identity,
                                                 bias=b3c[64:M13, 1:2]).then_inc(t3_ready, 1)
                        else:
                            nc.scalar.activation(t3[:, :], p3[(par + pos) % 2][:, :], ACT.Identity,
                                                 bias=b3c[:, pos:pos + 1]).then_inc(t3_ready, 1)
                    side(3 * pos + 1, k, par, half, moe, attn, norm, fin)
                    side(3 * pos + 2, k, par, half, moe, attn, norm, fin)
            act.wait_ge(setup_ev, 1)
            iterations(act, one)

        @block.vector
        def _(v):
            n = [0]

            def link(ins):
                n[0] += 1
                ins.then_inc(setup_dve, 1)
                v.wait_ge(setup_dve, n[0])

            nc.vector.memset(wsiT[:, N:P], 0.0)
            nc.vector.memset(aT[:, N:P], 0.0)
            nc.vector.memset(self_[64:P, :], 0.0)
            nc.vector.memset(self_[0:64, :], 1.0).then_inc(sel_ready, 1)
            nc.vector.memset(vrow[:, :], 0.0).then_inc(rows_zeroed, 1)
            nc.vector.memset(w2t[:, 1, :], 0.0).then_inc(w2_zeroed, 1)
            nc.vector.memset(w1f[:, HID + REST:HID + 64], 0.0)
            nc.vector.memset(sh1[:, :], 0.0)
            link(nc.vector.memset(hT[:, :], 1.0))
            nc.vector.memset(hT[0:N, step_cols(STEPS - 1)], 0.0)
            v.wait_ge(s_small, 16 * 8)
            link(nc.vector.tensor_tensor(out=wsi_t[:, :], in0=ws_t[:, :], in1=wi_t[:, :], op=ALU.add))
            v.wait_ge(setup_tr, 1)
            link(nc.vector.tensor_copy(vcol[:, :], pm[:, 320:352]))
            nc.vector.tensor_tensor(out=bu[:, :], in0=bsc, in1=bic, op=ALU.add)
            nc.vector.tensor_scalar(out=bgh[:, :], in0=bgc, scalar1=0.5, scalar2=None, op0=ALU.mult)
            nc.vector.tensor_copy(wsiT[:, 0:N], pm[:, 0:N])
            nc.vector.tensor_copy(woT[0:N, :], pm[0:N, 16:16 + D])
            nc.vector.tensor_copy(wgT[:, :], pm[:, 144:144 + D])
            nc.vector.tensor_copy(aT[:, 0:N], pm[0:N, 272:272 + N])
            link(nc.vector.tensor_copy(gwTh[:, :], pm[:, 288:288 + E]))
            nc.vector.tensor_tensor(out=gwTl[:, :], in0=pm[:, 288:288 + E], in1=gwTh[:, :].bitcast(fp32),
                                    op=ALU.subtract).then_inc(setup_ev, 1)

            def moments(w, src, tile):
                for q in range(Q):
                    ins = nc.vector.bn_stats(out=stats[w][:, q, :], in_=src[:, q, :])
                ins.then_inc(bn_done[w], 1)
                v.wait_ge(bn_done[w], tile + 1)
                nc.vector.memset(scratch[:, :], 0.0)
                for q in range(Q):
                    ins = nc.vector.bn_aggr(out=mv[w][:, q, :], in_=stats[w][:, q, :])
                ins.then_inc(mv_ready[w], 1)

            def normalize(w, src, dst, tile, ready):
                v.wait_ge(pool_r[w], 2 * tile + 2)
                for q in range(Q):
                    ins = nc.vector.tensor_scalar(out=dst[:, q, :], in0=src[:, q, :], scalar1=mv[w][:, q, 0:1],
                                                  scalar2=rstd[w][:, q:q + 1], op0=ALU.subtract, op1=ALU.mult)
                ins.then_inc(ready, 1)

            def bc(t):
                return t[:, :].unsqueeze(2).to_broadcast([P, Q, E])

            def router(tile, par1):
                r, e8 = row, ex8
                done = [0]

                def link(ins):
                    done[0] += 1
                    ins.then_inc(soft_step, 1)
                    v.wait_ge(soft_step, SOFT * tile + done[0])

                v.wait_ge(lg_ps, tile + 1)
                lg = pm[:, 0:Q * E].rearrange("p (q e) -> p q e", q=Q)
                link(nc.vector.tensor_reduce(out=r["max"][:, :], in_=lg, op=ALU.max, axis=AX.X))
                nc.vector.tensor_tensor(out=e8["ls"][:, :, :], in0=lg, in1=bc(r["max"]), op=ALU.subtract).then_inc(ls_ready, 1)
                v.wait_ge(ex_ready, tile + 1)
                link(nc.vector.tensor_reduce(out=r["sum"][:, :], in_=e8["ex"][:, :, :], op=ALU.add, axis=AX.X))
                link(nc.vector.reciprocal(r["inv"][:, :], r["sum"][:, :]))
                link(nc.vector.tensor_tensor(out=e8["sc"][:, :, :], in0=e8["ex"][:, :, :], in1=bc(r["inv"]), op=ALU.mult))
                gbb = gb[:, :].unsqueeze(1).to_broadcast([P, Q, E])
                revb = rev[:, :].unsqueeze(1).to_broadcast([P, Q, E])
                link(nc.vector.tensor_tensor(out=e8["bz"][:, :, :], in0=e8["sc"][:, :, :], in1=gbb, op=ALU.add))
                src = "bz"
                for m, i, cc, dd, o in (("m1", "i1", "c1", "d1", "o1"), ("m2", "i2", "c2", "d2", "o2")):
                    link(nc.vector.tensor_reduce(out=r[m][:, :], in_=e8[src][:, :, :], op=ALU.max, axis=AX.X))
                    link(nc.vector.tensor_tensor(out=e8[cc][:, :, :], in0=e8[src][:, :, :], in1=bc(r[m]), op=ALU.is_equal))
                    link(nc.vector.tensor_tensor(out=e8[dd][:, :, :], in0=e8[cc][:, :, :], in1=revb, op=ALU.mult))
                    link(nc.vector.tensor_reduce(out=r[i][:, :], in_=e8[dd][:, :, :], op=ALU.max, axis=AX.X))
                    link(nc.vector.tensor_tensor(out=e8[o][:, :, :], in0=e8[dd][:, :, :], in1=bc(r[i]), op=ALU.is_equal))
                    if src == "bz":
                        link(nc.vector.scalar_tensor_tensor(out=e8["bz2"][:, :, :], in0=e8["o1"][:, :, :], scalar=-1e30,
                                                            in1=e8["bz"][:, :, :], op0=ALU.mult, op1=ALU.add))
                        src = "bz2"
                link(nc.vector.tensor_tensor(out=e8["mk"][:, :, :], in0=e8["o1"][:, :, :], in1=e8["o2"][:, :, :], op=ALU.add))
                nc.vector.tensor_tensor(out=e8["rw"][:, :, :], in0=e8["mk"][:, :, :], in1=e8["sc"][:, :, :], op=ALU.mult)
                link(nc.vector.tensor_tensor(out=rwh[:, :, :], in0=e8["mk"][:, :, :], in1=e8["sc"][:, :, :], op=ALU.mult))
                wait(v, rwT_ps, tile)
                for at in (0, 64):
                    nc.vector.tensor_copy(rt[:, :, at:at + E], rwh[:, :, :].bitcast(fp32))
                    last = nc.vector.tensor_tensor(out=rt[:, :, at + 32:at + 32 + E], in0=e8["rw"][:, :, :],
                                                   in1=rwh[:, :, :].bitcast(fp32), op=ALU.subtract)
                last.then_inc(rt_ready, 1)
                assert done[0] == SOFT

            def side(slot, k, par, half, moe, attn, norm, fin):
                if slot == 7 and norm:
                    v.wait_ge(x_loaded[par], 16 * (half + 2))
                    moments("in", xt[par], k + 2)
                if slot == 9 and norm:
                    wait(v, xnT_ps, k + 2)
                    normalize("in", xt[par], xn, k + 2, xn_ready)
                if slot == 10 and fin:
                    v.wait_ge(y_ps, k)
                    wait(v, out_stored, 16 * (k - 1))
                    nc.vector.tensor_tensor(out=yo[:, :, :], in0=pm[:, :].rearrange("p (q d) -> p q d", q=Q),
                                            in1=x1[1 - par][:, :, :], op=ALU.add).then_inc(v2_ready, 1)
                    v.wait_ge(v2_ready, k)
                    moments("out", yo, k - 1)
                if slot == 13 and fin:
                    normalize("out", yo, yo, k - 1, yo_ready)
                if slot == 20 and attn:
                    v.wait_ge(ho_ps, k + 2)
                    v.wait_ge(gate_ready, k + 2)
                    nc.vector.scalar_tensor_tensor(out=og[:, :], in0=gth[1 - par][:, :], scalar=1.0, in1=pm[:, :],
                                                   op0=ALU.add, op1=ALU.mult).then_inc(og_ready, 1)
                if slot == 23 and attn:
                    v.wait_ge(ogT_ps, k + 2)
                    nc.vector.scalar_tensor_tensor(out=x1[1 - par][:, :, :], in0=xt[1 - par][:, :, :], scalar=4.0,
                                                   in1=pm[:, :].rearrange("p (q d) -> p q d", q=Q),
                                                   op0=ALU.mult, op1=ALU.add).then_inc(v_ready, 1)
                    v.wait_ge(v_ready, k + 2)
                    moments("mid", x1[1 - par], k + 1)
                if slot == 26 and attn:
                    normalize("mid", x1[1 - par], x1[1 - par], k + 1, x1_ready)
                if slot == 30 and attn:
                    v.wait_ge(x1h_ready, k + 2)
                    nc.vector.tensor_tensor(out=x1l[1 - par][:, :], in0=pm[:, :], in1=x1h[1 - par][:, :].bitcast(fp32),
                                            op=ALU.subtract).then_inc(x1l_ready, 1)
                if slot == 33 and attn:
                    router(k + 1, 1 - par)

            def weigh(pos, k):
                if pos < 2:
                    return
                v.wait_ge(sl_ready, POS * k + pos + 1)
                v.wait_ge(rwb_ps, CH * k + pos - 1)
                wait(v, down_ps, POS * k + pos - 2 if pos >= 5 else POS * k)
                nc.vector.tensor_tensor(out=st[pos % 3][:, :], in0=prw[:, :], in1=sl[pos % 2][:, :],
                                        op=ALU.mult).then_inc(s_ready, 1)

            def split_weights():
                v.wait_ge(s_big, 16 * 5)
                nc.vector.tensor_copy(w1h[:, :], w1f[:, :])
                link(nc.vector.tensor_copy(w3h[:, :], w3f[:, :]))
                nc.vector.tensor_tensor(out=w1l[:, :], in0=w1f[:, :], in1=w1h[:, :].bitcast(fp32), op=ALU.subtract)
                nc.vector.tensor_tensor(out=w3l[:, :], in0=w3f[:, :], in1=w3h[:, :].bitcast(fp32), op=ALU.subtract)
                v.wait_ge(const_made, 1)
                v.wait_ge(pool_step, 6)
                nc.vector.tensor_copy(sel[:, :], self_[:, :]).then_inc(setup_ev, 1)

            def one(k, par, half, moe, attn, norm, fin):
                if isinstance(k, int) and k == 0:
                    split_weights()
                for pos in range(POS):
                    if moe and pos >= 1:
                        weigh(pos - 1, k)
                    elif fin and pos == 0:
                        weigh(POS - 1, k - 1)
                    side(3 * pos, k, par, half, moe, attn, norm, fin)
                    if moe:
                        v.wait_ge(t3_ready, POS * k + pos + 1)
                        wait(v, sl_ready, POS * k + pos)
                        R = REST if pos == 1 else P
                        nc.vector.scalar_tensor_tensor(out=zt[0:R, :], in0=p1[(par + pos) % 2][0:R, :],
                                                       scalar=b1c[0:R, pos:pos + 1], in1=t3[0:R, :],
                                                       op0=ALU.add, op1=ALU.mult).then_inc(z_ready, 1)
                    side(3 * pos + 1, k, par, half, moe, attn, norm, fin)
                    side(3 * pos + 2, k, par, half, moe, attn, norm, fin)

            iterations(v, one)

        @block.tensor
        def _(pe):
            pe.wait_ge(id_made, 1)
            pe.wait_ge(setup_dve, 2)
            nc.tensor.transpose(pm[:, 0:N], wsi_t[:, :], ident[0:N, 0:N])
            nc.tensor.transpose(pm[0:N, 16:16 + D], wo_t[:, :], ident[:, :])
            pe.wait_ge(s_rows, 16 * 11)
            nc.tensor.transpose(pm[:, 320:352], vrow[:, :], ident[0:32, 0:32])
            nc.tensor.transpose(pm[:, 144:144 + D], wg_t[:, :], ident[:, :])
            nc.tensor.transpose(pm[0:N, 272:272 + N], a_t[:, :], ident[0:N, 0:N])
            nc.tensor.transpose(pm[:, 288:288 + E], gw_t[:, :], ident[0:E, 0:E]).then_inc(setup_tr, 1)

            def four_transposes(src, s):
                for q in range(Q):
                    ins = nc.tensor.transpose(pm[:, q * P:(q + 1) * P], src(q), ident[:, :])
                ins.then_inc(s, 1)

            def side(slot, k, par, half, moe, attn, norm, fin):
                if slot == 0 and attn:
                    pe.wait_ge(xnT_ready, k + 2)
                    wait(pe, h_ready, STEPS * (k + 1))
                    nc.tensor.matmul(pu[:, :], wsiT[:, :], xnT[:, :], start=True, stop=True,
                                     skip_group_check=True)
                if slot == 1 and moe:
                    pe.wait_ge(rt_ready, k + 1)
                    four_transposes(lambda q: rt[:, q, :], rwT_ps)
                if attn and 2 <= slot < 2 + STEPS:
                    t = slot - 2
                    c = step_cols(t)
                    n = STEPS * (k + 1) + t
                    wait(pe, h_ready, n)
                    nc.tensor.matmul(pu[:, c], aT[:, :], hT[0:N, step_cols((t - 1) % STEPS)], start=False,
                                     stop=True, skip_group_check=True).then_inc(h_ps, 1)
                if slot == 8 and fin:
                    pe.wait_ge(yT_ready, k)
                    if moe:
                        pe.wait_ge(rwT_ready, k + 1)
                    else:
                        wait(pe, v2_ready, k - 1)
                    four_transposes(lambda q: yT[:, q * P:(q + 1) * P], y_ps)
                if slot == 12 and norm:
                    pe.wait_ge(xn_ready, k + 3)
                    if fin:
                        pe.wait_ge(v2_ready, k)
                    elif moe:
                        pe.wait_ge(rwT_ready, k + 1)
                    else:
                        wait(pe, gate_ready, k + 2)
                    four_transposes(lambda q: xn[:, q, :], xnT_ps)
                if slot == 15 and norm:
                    pe.wait_ge(xnT_ready, k + 3)
                    nc.tensor.matmul(pm[:, :], wgT[:, :], xnT[:, :], start=True, stop=True).then_inc(gate_ps, 1)
                if slot == 19 and attn:
                    pe.wait_ge(h_ready, STEPS * (k + 2))
                    if norm:
                        pe.wait_ge(gate_ready, k + 3)
                    else:
                        pe.wait_ge(v2_ready, k)
                    nc.tensor.matmul(pm[:, :], woT[:, :], hT[:, :], start=True, stop=True).then_inc(ho_ps, 1)
                if slot == 22 and attn:
                    pe.wait_ge(og_ready, k + 2)
                    four_transposes(lambda q: og[:, q * P:(q + 1) * P], ogT_ps)
                if slot == 29 and attn:
                    pe.wait_ge(x1_ready, k + 2)
                    four_transposes(lambda q: x1[1 - par][:, q, :], x1T_ps)
                if slot == 32 and attn:
                    pe.wait_ge(x1l_ready, k + 2)
                    for q in range(Q):
                        qs = slice(q * P, (q + 1) * P)
                        o = pm[:, q * E:(q + 1) * E]
                        nc.tensor.matmul(o, x1l[1 - par][:, qs], gwTh[:, :], start=True, stop=False)
                        nc.tensor.matmul(o, x1h[1 - par][:, qs], gwTl[:, :], start=False, stop=False)
                        ins = nc.tensor.matmul(o, x1h[1 - par][:, qs], gwTh[:, :], start=False, stop=True)
                    ins.then_inc(lg_ps, 1)

            def broadcast(pos, k):
                if pos < 2:
                    return
                if pos == 2:
                    pe.wait_ge(rwT_ready, k + 1)
                wait(pe, s_ready, CH * k + pos - 2)
                nc.tensor.matmul(prw[:, :], sel[:, (pos - 2) * P:(pos - 1) * P], rwT[:, :],
                                 start=True, stop=True).then_inc(rwb_ps, 1)

            def split_product(o, wh, wl, par, done):
                nc.tensor.matmul(o, wl, x1h[par][:, :], start=True, stop=False)
                nc.tensor.matmul(o, wh, x1l[par][:, :], start=False, stop=False)
                ins = nc.tensor.matmul(o, wh, x1h[par][:, :], start=False, stop=True)
                if done is not None:
                    ins.then_inc(done, 1)

            def down(pos, k):
                if pos == 0:
                    wait(pe, yT_ready, k)
                if pos < 2:
                    pe.wait_ge(sl_ready, POS * k + pos + 1)
                else:
                    pe.wait_ge(s_ready, CH * k + pos - 1)
                nc.tensor.matmul(py[:, :], w2t[:, pos, :], s_tile(pos)[:, :], start=(pos == 0),
                                 stop=(pos == POS - 1)).then_inc(down_ps, 1)

            def one(k, par, half, moe, attn, norm, fin):
                if isinstance(k, int) and k == 0:
                    pe.wait_ge(setup_ev, 2)
                    pe.wait_ge(s_w2, 16 * 7)
                for pos in range(POS):
                    if moe and pos >= 1:
                        broadcast(pos - 1, k)
                    elif fin and pos == 0:
                        broadcast(POS - 1, k - 1)
                    if moe:
                        wait(pe, z_ready, POS * k + pos - 1)
                        bank = (par + pos) % 2
                        c = cols(pos)
                        o = p1[bank][0:c.stop - c.start, :]
                        split_product(o, w1h[:, c], w1l[:, c], par, up_ps if pos == 1 else None)
                    side(3 * pos, k, par, half, moe, attn, norm, fin)
                    if moe and pos != 1:
                        split_product(p3[bank][:, :], w3h[:, c], w3l[:, c], par, up_ps)
                    side(3 * pos + 1, k, par, half, moe, attn, norm, fin)
                    if moe and pos >= 2:
                        down(pos - 2, k)
                    elif fin and pos < 2:
                        down(POS - 2 + pos, k - 1)
                    side(3 * pos + 2, k, par, half, moe, attn, norm, fin)
            pe.wait_ge(setup_ev, 1)
            iterations(pe, one)


_INS = ["x", "Ws", "bs", "Wi", "bi", "Wo", "bo", "Wg", "bg", "ln_w", "ln_b", "A"]
_FFN = ["gate_w", "gate_b", "w1", "b1", "w3", "b3", "w2", "b2", "sw1", "sb1", "sw3", "sb3", "sw2", "sb2"]


def kernel(**inputs):
    import numpy as _np
    import concourse.bacc as _bacc
    from concourse import mybir as _mybir
    from concourse.bass_utils import run_bass_kernel_spmd as _run

    nc = _bacc.Bacc("TRN2", target_bir_lowering=False, num_devices=1)
    arrays, args = {}, []
    for name in [f"L0_attn_{n}" for n in _INS] + [f"L0_ffn_{n}" for n in _FFN]:
        a = _np.ascontiguousarray(inputs[name])
        arrays[f"in_{name}"] = a
        args.append(nc.dram_tensor(f"in_{name}", a.shape, _mybir.dt.from_np(a.dtype), kind="ExternalInput").ap())
    shape = arrays["in_L0_attn_x"].shape
    args.append(nc.dram_tensor("out", shape, _mybir.dt.float32, kind="ExternalOutput").ap())
    rnn_gate_moe_block(nc, *args)
    r = _run(nc, [arrays], core_ids=[0])
    return r.results[0]["out"]
```

```python
import concourse.bass as bass
from concourse import mybir
from contextlib import ExitStack


def rnn_gate_moe_block(nc, x, Ws, bs, Wi, bi, Wo, bo, Wg, bg, ln_w, ln_b, A,
                       gate_w, gate_b, w1, b1, w3, b3, w2, b2, sw1, sb1, sw3, sb3, sw2, sb2, out):
    fp32, fp32r = mybir.dt.float32, mybir.dt.float32r
    ALU, ACT, AX = mybir.AluOpType, mybir.ActivationFunctionType, mybir.AxisListType

    B, S, D = x.shape
    N = A.shape[0]
    E, _, H = w1.shape
    P = 128
    STEPS = 16
    TOK = B * STEPS
    Q = TOK // P
    TILES = S // STEPS
    CH = E * H // P
    REST = H - P
    POS = CH + 2
    HID = (CH + 1) * P
    M13 = 64 + REST
    EPS = 1e-5
    LAG = 6
    FULLS, PARTS = 4, 6
    SOFT = 11
    FILLER, TAKEN = -2e30, -1e30
    AT = dict(ho=1, xnT=2, gate=5, ogT=6, rwT=9, u=10, chain=11, x1T=15, yback=20, logits=23, yT=17,
              router_end=3, og=2, x1=7, norm_mid=12, moments_in=13, x1l=17, norm_in=18, v2=21, moments_out=22, router=24, kept=28, norm_out=30)
    AT_POOL = dict(mid=3, fresh=5, out=8, exp=9)
    NAPIER = 2.718281828459045

    xv = x.rearrange("b (k tq q) d -> k b tq (q d)", tq=STEPS // Q, q=Q)
    ov = out.rearrange("b (k tq q) d -> k b tq (q d)", tq=STEPS // Q, q=Q)

    with ExitStack() as ctx:
        def sb(name, shape, dt=fp32):
            return ctx.enter_context(nc.sbuf_tensor(name, shape, dt))

        def pb(name, shape=(P, TOK)):
            return ctx.enter_context(nc.psum_tensor(name, list(shape), fp32))

        def sem(name):
            return ctx.enter_context(nc.semaphore(name))

        ident = sb("ident", [P, P])
        neghalf = sb("neghalf", [P, Q])
        scratch = sb("scratch", [P, 1])
        eps1, eps4 = sb("eps1", [P, Q]), sb("eps4", [P, Q])
        primer = sb("primer", [P, Q])
        napier = sb("napier", [P, Q, E])
        ws_t, wi_t, wsi_t = sb("ws_t", [N, D]), sb("wi_t", [N, D]), sb("wsi_t", [N, D])
        wo_t = sb("wo_t", [D, N])
        vrow, vcol = sb("vrow", [32, P]), sb("vcol", [P, 32])
        wg_t, gw_t, a_t = sb("wg_t", [D, D]), sb("gw_t", [E, D]), sb("a_t", [N, N])
        wsiT, woT, wgT, aT = sb("wsiT", [D, N]), sb("woT", [N + 1, D]), sb("wgT", [D, D]), sb("aT", [P, N])
        gwT2 = sb("gwT2", [D, 2 * E], fp32r)
        bu, bgh = sb("bu", [N, 1]), sb("bgh", [D, 1])
        gb = sb("gb", [P, E])
        w1f, w3f = sb("w1f", [D, HID + M13]), sb("w3f", [D, HID])
        w1h, w1l = sb("w1h", [D, HID + M13], fp32r), sb("w1l", [D, HID + M13], fp32r)
        w3h, w3l = sb("w3h", [D, HID], fp32r), sb("w3l", [D, HID], fp32r)
        b1c, b3c = vcol[:, 0:POS], vcol[:, POS:2 * POS]
        bgc, lnw, lnb = (vcol[:, 2 * POS + i:2 * POS + i + 1] for i in range(3))
        bsc, bic = vcol[0:N, 29:30], vcol[0:N, 30:31]
        w2t = sb("w2t", [P, POS, D])
        w2h, w2l = sb("w2h", [P, POS, D], fp32r), sb("w2l", [P, POS, D], fp32r)
        self_, sel = sb("self_", [P, CH * P]), sb("sel", [P, CH * P], fp32r)

        xt = [sb(f"xt{i}", [P, Q, D]) for i in range(2)]
        xn = sb("xn", [P, Q, D])
        xnT = sb("xnT", [D, TOK])
        gth = [sb(f"gth{i}", [D, TOK]) for i in range(2)]
        hT = [sb(f"hT{i}", [P, TOK]) for i in range(2)]
        og = sb("og", [D, TOK])
        x1 = sb("x1", [P, Q, D])
        x1kept = [sb(f"x1kept{i}", [P, Q, D]) for i in range(2)]
        x1h = [sb(f"x1h{i}", [D, TOK], fp32r) for i in range(2)]
        x1l = [sb(f"x1l{i}", [D, TOK], fp32r) for i in range(2)]
        rwT = sb("rwT", [P, TOK], fp32r)
        rt = sb("rt", [P, Q, P])
        t3, zt = [sb(f"t3_{i}", [P, TOK]) for i in range(2)], [sb(f"zt{i}", [P, TOK]) for i in range(2)]
        sl = [sb(f"sl{i}", [P, TOK]) for i in range(2)]
        full = {w: sb(f"full_{w}", [P, TOK]) for w in ("sh0", "sh1", *range(FULLS))}
        high = {w: sb(f"high_{w}", [P, TOK], fp32r) for w in ("sh0", "sh1", *range(PARTS))}
        low = {w: sb(f"low_{w}", [P, TOK], fp32r) for w in ("sh0", "sh1", *range(PARTS))}
        yT = sb("yT", [D, TOK])
        yo = sb("yo", [P, Q, D])
        stats = {w: sb(f"stats_{w}", [P, Q, 6]) for w in ("in", "mid", "out")}
        mv = {w: sb(f"mv_{w}", [P, Q, 2]) for w in ("in", "mid", "out")}
        ve = {w: sb(f"ve_{w}", [P, Q]) for w in ("in", "mid", "out")}
        rstd = {w: sb(f"rstd_{w}", [P, Q]) for w in ("in", "mid", "out")}
        row = {w: sb(f"row_{w}", [P, Q]) for w in ("max", "sum", "inv")}
        ex8 = {w: sb(f"ex8_{w}", [P, Q, E]) for w in
               ("lg", "ls", "ex", "sc", "rw")}
        bz, taken = sb("bz", [P, Q, 2 * E]), sb("taken", [P, Q, 2 * E])
        top, best = sb("top", [P, Q, 8]), sb("best", [P, Q, 8])
        rwh = sb("rwh", [P, Q, E], fp32r)

        p1 = [pb(f"p1_{i}") for i in range(2)]
        p3 = [pb(f"p3_{i}") for i in range(2)]
        prw, py, pu, pm = pb("prw"), pb("py"), pb("pu"), pb("pm")

        s_rows, rows_zeroed = sem("s_rows"), sem("rows_zeroed")
        s_small, s_big, s_w2 = sem("s_small"), sem("s_big"), sem("s_w2")
        id_made, const_made, pool_step = sem("id_made"), sem("const_made"), sem("pool_step")
        w2_zeroed, setup_tr, setup_ev, setup_dve, sel_ready = (
            sem("w2_zeroed"), sem("setup_tr"), sem("setup_ev"), sem("setup_dve"), sem("sel_ready"))
        x_loaded = [sem("x_loaded0"), sem("x_loaded1")]
        out_stored = sem("out_stored")
        bn_done = {w: sem(f"bn_done_{w}") for w in ("in", "mid", "out")}
        mv_ready = {w: sem(f"mv_ready_{w}") for w in ("in", "mid", "out")}
        pool_r = {w: sem(f"pool_r_{w}") for w in ("in", "mid", "out")}
        xn_ready, xnT_ps, xnT_ready = sem("xn_ready"), sem("xnT_ps"), sem("xnT_ready")
        gate_ps, gate_ready = sem("gate_ps"), sem("gate_ready")
        h_ps, h_ready = sem("h_ps"), sem("h_ready")
        ho_ps, og_ready, ogT_ps, v_ready = sem("ho_ps"), sem("og_ready"), sem("ogT_ps"), sem("v_ready")
        x1_ready, x1T_ps, x1h_ready, x1l_ready = sem("x1_ready"), sem("x1T_ps"), sem("x1h_ready"), sem("x1l_ready")
        lg_ps, ls_ready, ex_ready, soft_step = sem("lg_ps"), sem("ls_ready"), sem("ex_ready"), sem("soft_step")
        rt_ready, rwT_ps, rwT_ready = sem("rt_ready"), sem("rwT_ps"), sem("rwT_ready")
        up_ps, t3_ready, z_ready, sl_ready = sem("up_ps"), sem("t3_ready"), sem("z_ready"), sem("sl_ready")
        rwb_ps, s_ready, down_ps = sem("rwb_ps"), sem("s_ready"), sem("down_ps")
        high_ready, low_ready = sem("high_ready"), sem("low_ready")
        yT_ready, y_ps, v2_ready, yo_ready = sem("yT_ready"), sem("y_ps"), sem("v2_ready"), sem("yo_ready")

        block = ctx.enter_context(nc.Block())

        def wait(eng, s, v):
            if not (isinstance(v, int) and v <= 0):
                eng.wait_ge(s, v)

        def iterations(eng, one):
            def straight(k):
                one(k, k % 2, k // 2, 0 <= k < TILES, 0 <= k + 1 < TILES, 0 <= k + 2 < TILES, k + 3 < TILES, 0 <= k - 1)
            for k in range(-3, 3):
                straight(k)
            with eng.Fori(0, (TILES - 6) // 2) as j:
                one(2 * j + 3, 1, j + 1, True, True, True, True, True)
                one(2 * j + 4, 0, j + 2, True, True, True, True, True)
            for k in range(TILES - 3, TILES + 1):
                straight(k)

        def cols(pos):
            if pos == 0:
                return slice(CH * P, HID)
            if pos == 1:
                return slice(HID, HID + M13)
            return slice((pos - 2) * P, (pos - 1) * P)

        def full_of(pos):
            return full[("sh0", "sh1")[pos]] if pos < 2 else full[pos % FULLS]

        def parts_of(pos):
            w = ("sh0", "sh1")[pos] if pos < 2 else pos % PARTS
            return high[w], low[w]

        def used(pos, k, turns):
            if pos < 2:
                return POS * (k - 1) + pos + 1
            if pos < 2 + turns:
                return POS * (k - 1) + max(p for p in range(2, POS) if p % turns == pos % turns) + 1
            return POS * k + pos - turns + 1

        def chain_step(slot):
            at = [AT['chain'] + t * 9 // 5 for t in range(STEPS)]
            return at.index(slot) if slot in at else None

        def step_cols(t):
            tq, q = divmod(t, Q)
            return slice(q * P + tq, (q + 1) * P, STEPS // Q)

        @block.sync
        def _(sp):
            for dst, src in ((ws_t, Ws), (wi_t, Wi), (a_t, A), (gw_t, gate_w), (wg_t, Wg), (wo_t, Wo)):
                sp.dma_start(dst[:, :], src).then_inc(s_small, 16)
            sp.dma_start(xt[0][:, :, :].rearrange("p q d -> p (q d)"), xv[0]).then_inc(x_loaded[0], 16)
            sp.dma_start(woT[N:N + 1, :], bo.rearrange("(a d) -> a d", a=1)).then_inc(s_small, 16)
            sp.dma_start(gb[:, :], gate_b.partition_broadcast(P)).then_inc(s_small, 16)
            sp.dma_start(xt[1][:, :, :].rearrange("p q d -> p (q d)"), xv[1]).then_inc(x_loaded[1], 16)
            sp.dma_start(w2t[:, 2:POS, :], w2.rearrange("e h d -> (e h) d").rearrange("(c p) d -> p c d", p=P)).then_inc(s_w2, 16)
            sp.dma_start(w2t[:, 0, :], sw2[0:P, :]).then_inc(s_w2, 16)
            sp.wait_ge(w2_zeroed, 1)
            sp.dma_start(w2t[0:REST, 1, :], sw2[P:H, :]).then_inc(s_w2, 16)
            for at in (64, 96):
                sp.dma_start(w2t[at:at + E, 1, :], b2).then_inc(s_w2, 16)
                sp.dma_start(w2t[at + E:at + E + 1, 1, :], sb2.rearrange("(a d) -> a d", a=1)).then_inc(s_w2, 16)

            def one(k, par, half, moe, attn, norm, pre, fin):
                if attn and (not isinstance(k, int) or k + 3 < TILES):
                    sp.wait_ge(v_ready, k + 2)
                    sp.dma_start(xt[1 - par][:, :, :].rearrange("p q d -> p (q d)"),
                                 xv[bass.ds(k + 3, 1)].rearrange("a b t f -> (a b) t f") if not isinstance(k, int) else xv[k + 3]
                                 ).then_inc(x_loaded[1 - par], 16)
                if fin:
                    sp.wait_ge(yo_ready, k)
                    sp.dma_start(ov[bass.ds(k - 1, 1)].rearrange("a b t f -> (a b) t f") if not isinstance(k, int) else ov[k - 1],
                                 yo[:, :, :].rearrange("p q d -> p (q d)")).then_inc(out_stored, 16)
            iterations(sp, one)
            sp.wait_ge(out_stored, 16 * TILES)

        @block.gpsimd
        def _(g):
            g.memset(ident[:, :], 0.0).then_inc(pool_step, 1)
            g.wait_ge(pool_step, 1)
            g.affine_select(out=ident[:, :], in_=ident[:, :], compare_op=ALU.not_equal, fill=1.0,
                            base=0, pattern=[[-1, P]], channel_multiplier=1).then_inc(id_made, 1)
            g.memset(neghalf[:, :], -0.5)
            g.memset(eps1[:, :], EPS)
            g.memset(eps4[:, :], 4 * EPS)
            g.memset(napier[:, :, :], NAPIER)
            g.memset(bz[:, :, E:2 * E], FILLER)
            g.memset(best[:, :, 2:8], FILLER)
            g.memset(rt[:, :, :], 0.0).then_inc(pool_step, 1)
            g.wait_ge(pool_step, 2)
            g.memset(rt[:, :, E:E + 1], 1.0)
            g.memset(rt[:, :, 64 + E:65 + E], 1.0).then_inc(const_made, 1)
            g.wait_ge(const_made, 1)
            g.wait_ge(sel_ready, 1)
            n = 2
            for r in (0, 32):
                v = self_[r:r + 32, :]
                g.affine_select(out=v, in_=v, compare_op=ALU.is_ge, fill=0.0,
                                base=0, pattern=[[1, CH * P]], channel_multiplier=-H).then_inc(pool_step, 1)
                n += 1
                g.wait_ge(pool_step, n)
                g.affine_select(out=v, in_=v, compare_op=ALU.is_ge, fill=0.0,
                                base=H - 1, pattern=[[-1, CH * P]], channel_multiplier=H).then_inc(pool_step, 1)
                n += 1
                g.wait_ge(pool_step, n)

            def rsqrt(w, tile, eps_t):
                g.wait_ge(mv_ready[w], tile + 1)
                g.tensor_tensor(out=ve[w][:, :], in0=mv[w][:, :, 1], in1=eps_t[:, :], op=ALU.add).then_inc(pool_r[w], 1)
                g.wait_ge(pool_r[w], 2 * tile + 1)
                g.tensor_tensor(out=rstd[w][:, :], in0=ve[w][:, :], in1=neghalf[:, :], op=ALU.pow).then_inc(pool_r[w], 1)

            def low_part(pos, k):
                R = REST if pos == 1 else P
                hi, lo = parts_of(pos)
                g.wait_ge(high_ready, POS * k + pos + 1)
                g.tensor_tensor(out=lo[0:R, :], in0=full_of(pos)[0:R, :], in1=hi[0:R, :].bitcast(fp32),
                                op=ALU.subtract).then_inc(low_ready, 1)

            def one(k, par, half, moe, attn, norm, pre, fin):
                for pos in range(POS):
                    if pos == AT_POOL['mid'] and attn:
                        rsqrt("mid", k + 1, eps4)
                    if pos == AT_POOL['out'] and fin:
                        rsqrt("out", k - 1, eps1)
                    if pos == AT_POOL['fresh'] and pre:
                        rsqrt("in", k + 3, eps1)
                    if AT_POOL['exp'] <= pos < AT_POOL['exp'] + Q and attn:
                        g.wait_ge(ls_ready, k + 2)
                        q = pos - AT_POOL['exp']
                        g.tensor_tensor(out=ex8["ex"][:, q, :], in0=napier[:, q, :], in1=ex8["ls"][:, q, :],
                                        op=ALU.pow).then_inc(ex_ready, 1)
                    if moe and pos >= 2:
                        low_part(pos - 2, k)
                    elif fin and pos < 2:
                        low_part(POS - 2 + pos, k - 1)
            iterations(g, one)

        @block.scalar
        def _(act):
            act.wait_ge(rows_zeroed, 1)
            for r, at, src, ssrc in ((0, 0, b1, sb1), (POS, 64, b3, sb3)):
                act.dma_start(vrow[r + 2:r + POS, :], src.rearrange("e h -> (e h)").rearrange("(c p) -> c p", p=P)).then_inc(s_rows, 16)
                act.dma_start(vrow[r:r + 1, :], ssrc[0:P].rearrange("(a d) -> a d", a=1)).then_inc(s_rows, 16)
                act.dma_start(vrow[r + 1:r + 2, at:at + REST], ssrc[P:H].rearrange("(a d) -> a d", a=1)).then_inc(s_rows, 16)
            for r, src in enumerate((bg, ln_w, ln_b, bs, bi)):
                act.dma_start(vrow[2 * POS + r:2 * POS + r + 1, 0:src.shape[0]], src.rearrange("(a d) -> a d", a=1)).then_inc(s_rows, 16)
            act.dma_start(w1f[:, 0:CH * P].rearrange("d (e h) -> d e h", e=E), w1.rearrange("e d h -> d e h")).then_inc(s_big, 16)
            act.dma_start(w3f[:, 0:CH * P].rearrange("d (e h) -> d e h", e=E), w3.rearrange("e d h -> d e h")).then_inc(s_big, 16)
            act.dma_start(w1f[:, CH * P:HID + REST], sw1).then_inc(s_big, 16)
            act.dma_start(w3f[:, CH * P:HID], sw3[:, 0:P]).then_inc(s_big, 16)
            act.dma_start(w1f[:, HID + 64:HID + M13], sw3[:, P:H]).then_inc(s_big, 16)
            act.wait_ge(const_made, 1)
            nc.scalar.activation(primer[:, :], neghalf[:, :], ACT.Silu)

            def side(slot, k, par, half, moe, attn, norm, pre, fin):
                t = chain_step(slot)
                if norm and t is not None:
                    c = step_cols(t)
                    act.wait_ge(h_ps, STEPS * (k + 2) + t + 1)
                    nc.scalar.activation(hT[par][0:N, c], pu[0:N, c], ACT.Tanh, bias=bu[:, 0:1]).then_inc(h_ready, 1)
                if slot == AT['rwT'] and moe:
                    act.wait_ge(rwT_ps, k + 1)
                    nc.scalar.activation(rwT[:, :], pm[:, :], ACT.Identity)
                    nc.scalar.activation(high["sh1"][64:P, :], pm[64:P, :], ACT.Identity).then_inc(rwT_ready, 1)
                if slot == AT['yT'] and fin:
                    act.wait_ge(down_ps, POS * k)
                    wait(act, y_ps, k - 1)
                    nc.scalar.activation(yT[:, :], py[:, :], ACT.Identity).then_inc(yT_ready, 1)
                if slot == AT['xnT'] and norm:
                    act.wait_ge(xnT_ps, k + 3)
                    nc.scalar.activation(xnT[:, :], pm[:, :], ACT.Identity, scale=lnw,
                                         bias=lnb).then_inc(xnT_ready, 1)
                if slot == AT['gate'] and norm:
                    act.wait_ge(gate_ps, k + 3)
                    wait(act, og_ready, k + 1)
                    nc.scalar.activation(gth[par][:, :], pm[:, :], ACT.Tanh, scale=0.5,
                                         bias=bgh[:, 0:1]).then_inc(gate_ready, 1)
                if slot == AT['x1T'] + 1 and attn:
                    act.wait_ge(x1T_ps, k + 2)
                    nc.scalar.activation(x1h[1 - par][:, :], pm[:, :], ACT.Identity).then_inc(x1h_ready, 1)

            def silu(pos, par, k):
                act.wait_ge(z_ready, POS * k + pos + 1)
                if pos < 2:
                    R = REST if pos == 1 else P
                    wait(act, low_ready, POS * (k - 1) + pos + 1)
                    nc.scalar.activation(full_of(pos)[0:R, :], zt[(par + pos) % 2][0:R, :], ACT.Silu).then_inc(sl_ready, 1)
                else:
                    wait(act, s_ready, CH * k + max(pos - 3, 0))
                    nc.scalar.activation(sl[pos % 2][:, :], zt[(par + pos) % 2][:, :], ACT.Silu).then_inc(sl_ready, 1)

            def high_part(pos, k):
                R = REST if pos == 1 else P
                if pos < 2:
                    act.wait_ge(sl_ready, POS * k + pos + 1)
                else:
                    act.wait_ge(s_ready, CH * k + pos - 1)
                wait(act, down_ps, used(pos, k, PARTS))
                nc.scalar.activation(parts_of(pos)[0][0:R, :], full_of(pos)[0:R, :], ACT.Identity).then_inc(high_ready, 1)

            def one(k, par, half, moe, attn, norm, pre, fin):
                for pos in range(POS):
                    side(3 * pos, k, par, half, moe, attn, norm, pre, fin)
                    if moe:
                        act.wait_ge(up_ps, POS * k + pos + 1)
                        if pos == 1:
                            nc.scalar.activation(t3[par ^ 1][0:REST, :], p1[par ^ 1][64:M13, :], ACT.Identity,
                                                 bias=b3c[64:M13, 1:2]).then_inc(t3_ready, 1)
                        else:
                            nc.scalar.activation(t3[(par + pos) % 2][:, :], p3[(par + pos) % 2][:, :], ACT.Identity,
                                                 bias=b3c[:, pos:pos + 1]).then_inc(t3_ready, 1)
                    side(3 * pos + 1, k, par, half, moe, attn, norm, pre, fin)
                    if moe and pos >= 1:
                        silu(pos - 1, par, k)
                    elif fin and pos == 0:
                        silu(POS - 1, 1 - par, k - 1)
                    side(3 * pos + 2, k, par, half, moe, attn, norm, pre, fin)
                    if moe and pos >= 2:
                        high_part(pos - 2, k)
                    elif fin and pos < 2:
                        high_part(POS - 2 + pos, k - 1)
            act.wait_ge(setup_ev, 1)
            iterations(act, one)

        @block.vector
        def _(v):
            n = [0]

            def link(ins):
                n[0] += 1
                ins.then_inc(setup_dve, 1)
                v.wait_ge(setup_dve, n[0])

            link(nc.vector.memset(aT[:, :], 0.0))
            nc.vector.memset(self_[64:P, :], 0.0)
            nc.vector.memset(self_[0:64, :], 1.0).then_inc(sel_ready, 1)
            nc.vector.memset(vrow[:, :], 0.0).then_inc(rows_zeroed, 1)
            nc.vector.memset(w2t[:, 1, :], 0.0).then_inc(w2_zeroed, 1)
            nc.vector.memset(w1f[:, HID + REST:HID + 64], 0.0)
            nc.vector.memset(high["sh1"][:, :].bitcast(fp32), 0.0)
            nc.vector.memset(low["sh1"][:, :].bitcast(fp32), 0.0)
            nc.vector.memset(hT[0][:, :], 1.0)
            link(nc.vector.memset(hT[1][:, :], 1.0))
            link(nc.vector.memset(hT[1][0:N, step_cols(STEPS - 1)], 0.0))
            v.wait_ge(s_small, 16 * 8)
            link(nc.vector.tensor_tensor(out=wsi_t[:, :], in0=ws_t[:, :], in1=wi_t[:, :], op=ALU.add))
            v.wait_ge(setup_tr, 1)
            link(nc.vector.tensor_copy(vcol[:, :], pm[:, 320:352]))
            nc.vector.tensor_tensor(out=bu[:, :], in0=bsc, in1=bic, op=ALU.add)
            nc.vector.tensor_scalar(out=bgh[:, :], in0=bgc, scalar1=0.5, scalar2=None, op0=ALU.mult)
            nc.vector.tensor_copy(wsiT[:, 0:N], pm[:, 0:N])
            nc.vector.tensor_copy(woT[0:N, :], pm[0:N, 16:16 + D])
            nc.vector.tensor_copy(wgT[:, :], pm[:, 144:144 + D])
            nc.vector.tensor_copy(aT[0:N, :], pm[0:N, 272:272 + N])
            link(nc.vector.tensor_copy(gwT2[:, 0:E], pm[:, 288:288 + E]))
            nc.vector.tensor_tensor(out=gwT2[:, E:2 * E], in0=pm[:, 288:288 + E], in1=gwT2[:, 0:E].bitcast(fp32),
                                    op=ALU.subtract).then_inc(setup_ev, 1)

            def moments(w, src, tile):
                for q in range(Q):
                    ins = nc.vector.bn_stats(out=stats[w][:, q, :], in_=src[:, q, :])
                ins.then_inc(bn_done[w], 1)
                v.wait_ge(bn_done[w], tile + 1)
                nc.vector.memset(scratch[:, :], 0.0)
                for q in range(Q):
                    ins = nc.vector.bn_aggr(out=mv[w][:, q, :], in_=stats[w][:, q, :])
                ins.then_inc(mv_ready[w], 1)

            def normalize(w, src, dst, tile, ready):
                v.wait_ge(pool_r[w], 2 * tile + 2)
                for q in range(Q):
                    ins = nc.vector.tensor_scalar(out=dst[:, q, :], in0=src[:, q, :], scalar1=mv[w][:, q, 0:1],
                                                  scalar2=rstd[w][:, q:q + 1], op0=ALU.subtract, op1=ALU.mult)
                ins.then_inc(ready, 1)

            def bc(t):
                return t[:, :].unsqueeze(2).to_broadcast([P, Q, E])

            def router(step, tile):
                r, e8 = row, ex8
                lg = e8["lg"][:, :, :]
                gbb = gb[:, :].unsqueeze(1).to_broadcast([P, Q, E])
                tt = nc.vector.tensor_tensor

                if step == 0:
                    v.wait_ge(lg_ps, tile + 1)
                    ins = nc.vector.tensor_reduce(out=lg, in_=pm[:, 0:2 * Q * E].rearrange("p (q s e) -> p q e s", q=Q, s=2),
                                                  op=ALU.add, axis=AX.X)
                else:
                    v.wait_ge(soft_step, SOFT * tile + step)
                if step == 1:
                    ins = nc.vector.tensor_reduce(out=r["max"][:, :], in_=lg, op=ALU.max, axis=AX.X)
                if step == 2:
                    ins = tt(out=e8["ls"][:, :, :], in0=lg, in1=bc(r["max"]), op=ALU.subtract)
                    ins.then_inc(ls_ready, 1)
                    ins = nc.vector.memset(scratch[:, :], 0.0)
                if step == 3:
                    v.wait_ge(ex_ready, Q * (tile + 1))
                    ins = nc.vector.tensor_reduce(out=r["sum"][:, :], in_=e8["ex"][:, :, :], op=ALU.add, axis=AX.X)
                if step == 4:
                    ins = nc.vector.reciprocal(r["inv"][:, :], r["sum"][:, :])
                if step == 5:
                    ins = tt(out=e8["sc"][:, :, :], in0=e8["ex"][:, :, :], in1=bc(r["inv"]), op=ALU.mult)
                if step == 6:
                    ins = tt(out=bz[:, :, 0:E], in0=e8["sc"][:, :, :], in1=gbb, op=ALU.add)
                if step == 7:
                    nc.vector.memset(scratch[:, :], 0.0)
                    for q in range(Q):
                        ins = nc.vector.max(out=top[:, q, :], in_=bz[:, q, 0:E])
                if step == 8:
                    ins = nc.vector.tensor_copy(best[:, :, 0:2], top[:, :, 0:2])
                if step == 9:
                    nc.vector.memset(scratch[:, :], 0.0)
                    for q in range(Q):
                        ins = nc.vector.match_replace(out=taken[:, q, :], in_to_replace=best[:, q, :],
                                                      in_values=bz[:, q, :], imm_value=TAKEN)
                if step == 10:
                    for dst in (e8["rw"], rwh):
                        ins = nc.vector.scalar_tensor_tensor(out=dst[:, :, :], in0=taken[:, :, 0:E], scalar=TAKEN,
                                                             in1=e8["sc"][:, :, :], op0=ALU.is_equal, op1=ALU.mult)
                if step < SOFT:
                    ins.then_inc(soft_step, 1)
                else:
                    wait(v, rwT_ps, tile)
                    for at in (0, 64):
                        nc.vector.tensor_copy(rt[:, :, at:at + E], rwh[:, :, :].bitcast(fp32))
                        last = tt(out=rt[:, :, at + 32:at + 32 + E], in0=e8["rw"][:, :, :],
                                  in1=rwh[:, :, :].bitcast(fp32), op=ALU.subtract)
                    last.then_inc(rt_ready, 1)

            def side(slot, k, par, half, moe, attn, norm, pre, fin):
                if moe and 0 <= slot - AT['router_end'] < 5:
                    for step in range(3, SOFT + 1)[2 * (slot - AT['router_end']):2 * (slot - AT['router_end']) + 2]:
                        router(step, k)
                if slot == AT['og'] and attn:
                    v.wait_ge(ho_ps, k + 2)
                    v.wait_ge(gate_ready, k + 2)
                    nc.vector.scalar_tensor_tensor(out=og[:, :], in0=gth[1 - par][:, :], scalar=1.0, in1=pu[:, :],
                                                   op0=ALU.add, op1=ALU.mult).then_inc(og_ready, 1)
                if slot == AT['x1'] and attn:
                    v.wait_ge(ogT_ps, k + 2)
                    nc.vector.scalar_tensor_tensor(out=x1[:, :, :], in0=xt[1 - par][:, :, :], scalar=4.0,
                                                   in1=pu[:, :].rearrange("p (q d) -> p q d", q=Q),
                                                   op0=ALU.mult, op1=ALU.add).then_inc(v_ready, 1)
                    v.wait_ge(v_ready, k + 2)
                    moments("mid", x1, k + 1)
                if slot == AT['norm_mid'] and attn:
                    normalize("mid", x1, x1, k + 1, x1_ready)
                if slot == AT['x1l'] and attn:
                    v.wait_ge(x1h_ready, k + 2)
                    nc.vector.tensor_tensor(out=x1l[1 - par][:, :], in0=pm[:, :], in1=x1h[1 - par][:, :].bitcast(fp32),
                                            op=ALU.subtract).then_inc(x1l_ready, 1)
                if attn and slot in range(AT['router'], AT['router'] + 3):
                    router(slot - AT['router'], k + 1)
                if slot == AT['v2'] and fin:
                    v.wait_ge(y_ps, k)
                    wait(v, out_stored, 16 * (k - 1))
                    nc.vector.tensor_tensor(out=yo[:, :, :], in0=pm[:, :].rearrange("p (q d) -> p q d", q=Q),
                                            in1=x1kept[1 - par][:, :, :], op=ALU.add).then_inc(v2_ready, 1)
                if slot == AT['moments_out'] and fin:
                    v.wait_ge(v2_ready, k)
                    moments("out", yo, k - 1)
                if slot == AT['kept'] and attn:
                    v.wait_ge(x1_ready, k + 2)
                    nc.vector.tensor_copy(x1kept[1 - par][:, :, :], x1[:, :, :])
                if slot == AT['moments_in'] and pre:
                    v.wait_ge(x_loaded[1 - par], 16 * (half + 2 + par))
                    moments("in", xt[1 - par], k + 3)
                if slot == AT['norm_out'] and fin:
                    normalize("out", yo, yo, k - 1, yo_ready)
                if slot == AT['norm_in'] and pre:
                    wait(v, xnT_ps, k + 3)
                    normalize("in", xt[1 - par], xn, k + 3, xn_ready)

            def weigh(pos, k):
                if pos < 2:
                    return
                v.wait_ge(sl_ready, POS * k + pos + 1)
                v.wait_ge(rwb_ps, CH * k + pos - 1)
                wait(v, low_ready, used(pos, k, FULLS))
                nc.vector.tensor_tensor(out=full_of(pos)[:, :], in0=prw[:, :], in1=sl[pos % 2][:, :],
                                        op=ALU.mult).then_inc(s_ready, 1)

            def split_weights():
                v.wait_ge(s_big, 16 * 5)
                v.wait_ge(s_w2, 16 * 7)
                nc.vector.tensor_copy(w1h[:, :], w1f[:, :])
                nc.vector.tensor_copy(w2h[:, :, :], w2t[:, :, :])
                link(nc.vector.tensor_copy(w3h[:, :], w3f[:, :]))
                nc.vector.tensor_tensor(out=w1l[:, :], in0=w1f[:, :], in1=w1h[:, :].bitcast(fp32), op=ALU.subtract)
                nc.vector.tensor_tensor(out=w3l[:, :], in0=w3f[:, :], in1=w3h[:, :].bitcast(fp32), op=ALU.subtract)
                nc.vector.tensor_tensor(out=w2l[:, :, :], in0=w2t[:, :, :], in1=w2h[:, :, :].bitcast(fp32), op=ALU.subtract)
                v.wait_ge(const_made, 1)
                v.wait_ge(pool_step, 6)
                nc.vector.tensor_copy(sel[:, :], self_[:, :]).then_inc(setup_ev, 1)

            def one(k, par, half, moe, attn, norm, pre, fin):
                if isinstance(k, int) and k == 0:
                    split_weights()
                for pos in range(POS):
                    side(3 * pos, k, par, half, moe, attn, norm, pre, fin)
                    if moe:
                        v.wait_ge(t3_ready, POS * k + pos + 1)
                        wait(v, sl_ready, POS * k + pos - 1)
                        R = REST if pos == 1 else P
                        nc.vector.scalar_tensor_tensor(out=zt[(par + pos) % 2][0:R, :], in0=p1[(par + pos) % 2][0:R, :],
                                                       scalar=b1c[0:R, pos:pos + 1], in1=t3[(par + pos) % 2][0:R, :],
                                                       op0=ALU.add, op1=ALU.mult).then_inc(z_ready, 1)
                    side(3 * pos + 1, k, par, half, moe, attn, norm, pre, fin)
                    side(3 * pos + 2, k, par, half, moe, attn, norm, pre, fin)
                    if moe and pos >= 1:
                        weigh(pos - 1, k)
                    elif fin and pos == 0:
                        weigh(POS - 1, k - 1)

            iterations(v, one)

        @block.tensor
        def _(pe):
            pe.wait_ge(id_made, 1)
            pe.wait_ge(setup_dve, 4)
            nc.tensor.transpose(pm[:, 0:N], wsi_t[:, :], ident[0:N, 0:N])
            nc.tensor.transpose(pm[0:N, 16:16 + D], wo_t[:, :], ident[:, :])
            pe.wait_ge(s_rows, 16 * 11)
            nc.tensor.transpose(pm[:, 320:352], vrow[:, :], ident[0:32, 0:32])
            nc.tensor.transpose(pm[:, 144:144 + D], wg_t[:, :], ident[:, :])
            nc.tensor.transpose(pm[0:N, 272:272 + N], a_t[:, :], ident[0:N, 0:N])
            nc.tensor.transpose(pm[:, 288:288 + E], gw_t[:, :], ident[0:E, 0:E]).then_inc(setup_tr, 1)

            def four_transposes(bank, src, s):
                for q in range(Q):
                    ins = nc.tensor.transpose(bank[:, q * P:(q + 1) * P], src(q), ident[:, :])
                ins.then_inc(s, 1)

            def side(slot, k, par, half, moe, attn, norm, pre, fin):
                if slot == AT['xnT'] and norm:
                    pe.wait_ge(xn_ready, k + 3)
                    four_transposes(pm, lambda q: xn[:, q, :], xnT_ps)
                if slot == AT['ho'] and attn:
                    pe.wait_ge(h_ready, STEPS * (k + 2))
                    nc.tensor.matmul(pu[:, :], woT[:, :], hT[1 - par][0:N + 1, :], start=True, stop=True).then_inc(ho_ps, 1)
                if slot == AT['gate'] and norm:
                    pe.wait_ge(xnT_ready, k + 3)
                    nc.tensor.matmul(pm[:, :], wgT[:, :], xnT[:, :], start=True, stop=True).then_inc(gate_ps, 1)
                if slot == AT['ogT'] and attn:
                    pe.wait_ge(og_ready, k + 2)
                    four_transposes(pu, lambda q: og[:, q * P:(q + 1) * P], ogT_ps)
                if slot == AT['rwT'] and moe:
                    pe.wait_ge(rt_ready, k + 1)
                    if norm:
                        pe.wait_ge(gate_ready, k + 3)
                    else:
                        pe.wait_ge(v2_ready, k - 1)
                    four_transposes(pm, lambda q: rt[:, q, :], rwT_ps)
                if slot == AT['u'] and norm:
                    pe.wait_ge(xnT_ready, k + 3)
                    if attn:
                        pe.wait_ge(v_ready, k + 2)
                    nc.tensor.matmul(pu[0:N, :], wsiT[:, :], xnT[:, :], start=True, stop=True, skip_group_check=True)
                t = chain_step(slot)
                if norm and t is not None:
                    c = step_cols(t)
                    before = hT[par if t else 1 - par][:, step_cols((t - 1) % STEPS)]
                    wait(pe, h_ready, STEPS * (k + 2) + t)
                    nc.tensor.matmul(pu[0:N, c], aT[:, :], before, start=False, stop=True,
                                     skip_group_check=True).then_inc(h_ps, 1)
                if slot == AT['x1T'] and attn:
                    pe.wait_ge(x1_ready, k + 2)
                    if moe:
                        pe.wait_ge(rwT_ready, k + 1)
                    elif norm:
                        pe.wait_ge(gate_ready, k + 3)
                    four_transposes(pm, lambda q: x1[:, q, :], x1T_ps)
                if slot == AT['logits'] and attn:
                    pe.wait_ge(x1l_ready, k + 2)
                    wait(pe, v2_ready, k)
                    for q in range(Q):
                        qs = slice(q * P, (q + 1) * P)
                        o = pm[:, 2 * q * E:2 * (q + 1) * E]
                        nc.tensor.matmul(o, x1h[1 - par][:, qs], gwT2[:, :], start=True, stop=False, skip_group_check=True)
                        ins = nc.tensor.matmul(o[:, 0:E], x1l[1 - par][:, qs], gwT2[:, 0:E], start=False, stop=True,
                                               skip_group_check=True)
                    ins.then_inc(lg_ps, 1)
                if slot == AT['yback'] and fin:
                    pe.wait_ge(yT_ready, k)
                    if attn:
                        pe.wait_ge(x1l_ready, k + 2)
                    elif moe:
                        pe.wait_ge(rwT_ready, k + 1)
                    else:
                        pe.wait_ge(v2_ready, k - 1)
                    four_transposes(pm, lambda q: yT[:, q * P:(q + 1) * P], y_ps)

            def broadcast(pos, k):
                if pos < 2:
                    return
                if pos == 2:
                    pe.wait_ge(rwT_ready, k + 1)
                wait(pe, s_ready, CH * k + pos - 2)
                nc.tensor.matmul(prw[:, :], sel[:, (pos - 2) * P:(pos - 1) * P], rwT[:, :],
                                 start=True, stop=True).then_inc(rwb_ps, 1)

            def split_product(o, wh, wl, par, done):
                nc.tensor.matmul(o, wl, x1h[par][:, :], start=True, stop=False)
                nc.tensor.matmul(o, wh, x1l[par][:, :], start=False, stop=False)
                ins = nc.tensor.matmul(o, wh, x1h[par][:, :], start=False, stop=True)
                if done is not None:
                    ins.then_inc(done, 1)

            def down(pos, k):
                if pos == 0:
                    wait(pe, yT_ready, k)
                pe.wait_ge(low_ready, POS * k + pos + 1)
                hi, lo = parts_of(pos)
                nc.tensor.matmul(py[:, :], w2h[:, pos, :], lo[:, :], start=(pos == 0), stop=False)
                nc.tensor.matmul(py[:, :], w2l[:, pos, :], hi[:, :], start=False, stop=False)
                nc.tensor.matmul(py[:, :], w2h[:, pos, :], hi[:, :], start=False,
                                 stop=(pos == POS - 1)).then_inc(down_ps, 1)

            def one(k, par, half, moe, attn, norm, pre, fin):
                if isinstance(k, int) and k == 0:
                    pe.wait_ge(setup_ev, 2)
                for pos in range(POS):
                    if moe:
                        wait(pe, z_ready, POS * k + pos - 1)
                        bank = (par + pos) % 2
                        c = cols(pos)
                        o = p1[bank][0:c.stop - c.start, :]
                        split_product(o, w1h[:, c], w1l[:, c], par, up_ps if pos == 1 else None)
                    side(3 * pos, k, par, half, moe, attn, norm, pre, fin)
                    if moe and pos != 1:
                        split_product(p3[bank][:, :], w3h[:, c], w3l[:, c], par, up_ps)
                    side(3 * pos + 1, k, par, half, moe, attn, norm, pre, fin)
                    if moe and pos >= LAG:
                        down(pos - LAG, k)
                    elif fin and pos < LAG:
                        down(POS - LAG + pos, k - 1)
                    if moe and pos >= 1:
                        broadcast(pos - 1, k)
                    elif fin and pos == 0:
                        broadcast(POS - 1, k - 1)
                    side(3 * pos + 2, k, par, half, moe, attn, norm, pre, fin)
            pe.wait_ge(setup_ev, 1)
            iterations(pe, one)


_INS = ["x", "Ws", "bs", "Wi", "bi", "Wo", "bo", "Wg", "bg", "ln_w", "ln_b", "A"]
_FFN = ["gate_w", "gate_b", "w1", "b1", "w3", "b3", "w2", "b2", "sw1", "sb1", "sw3", "sb3", "sw2", "sb2"]


def kernel(**inputs):
    import numpy as _np
    import concourse.bacc as _bacc
    from concourse import mybir as _mybir
    from concourse.bass_utils import run_bass_kernel_spmd as _run

    nc = _bacc.Bacc("TRN2", target_bir_lowering=False, num_devices=1)
    arrays, args = {}, []
    for name in [f"L0_attn_{n}" for n in _INS] + [f"L0_ffn_{n}" for n in _FFN]:
        a = _np.ascontiguousarray(inputs[name])
        arrays[f"in_{name}"] = a
        args.append(nc.dram_tensor(f"in_{name}", a.shape, _mybir.dt.from_np(a.dtype), kind="ExternalInput").ap())
    shape = arrays["in_L0_attn_x"].shape
    args.append(nc.dram_tensor("out", shape, _mybir.dt.float32, kind="ExternalOutput").ap())
    rnn_gate_moe_block(nc, *args)
    r = _run(nc, [arrays], core_ids=[0])
    return r.results[0]["out"]
```

```python
import concourse.bass as bass
from concourse import mybir
from contextlib import ExitStack


def rnn_gate_moe_block(nc, x, Ws, bs, Wi, bi, Wo, bo, Wg, bg, ln_w, ln_b, A,
                       gate_w, gate_b, w1, b1, w3, b3, w2, b2, sw1, sb1, sw3, sb3, sw2, sb2, out):
    fp32, fp32r = mybir.dt.float32, mybir.dt.float32r
    ALU, ACT, AX = mybir.AluOpType, mybir.ActivationFunctionType, mybir.AxisListType

    B, S, D = x.shape
    N = A.shape[0]
    E, _, H = w1.shape
    P = 128
    STEPS = 16
    TOK = B * STEPS
    Q = TOK // P
    TILES = S // STEPS
    CH = E * H // P
    REST = H - P
    POS = CH + 2
    HID = (CH + 1) * P
    M13 = 64 + REST
    EPS = 1e-5
    LAG = 5
    FULLS, PARTS = 4, 6
    SOFT = 11
    FILLER, TAKEN = -2e30, -1e30
    AT = dict(ho=1, xnT=2, gate=5, ogT=6, rwT=10, u=10, chain=11, x1T=15, yback=20, logits=23, yT=14,
              router_end=2, og=2, x1=7, norm_mid=12, moments_in=13, x1l=17, norm_in=18, v2=21, moments_out=22,
              router=24, kept=28, norm_out=30)
    AT_START = dict(xnT=2, gate=6, u=3, chain=4, ogT=4, x1T=12, x1l=14, logits=15, router=16,
                    second_xnT=9, second_gate=14)
    AT_POOL = dict(mid=3, fresh=5, out=8, exp=9)
    NAPIER = 2.718281828459045

    xv = x.rearrange("b (k tq q) d -> k b tq (q d)", tq=STEPS // Q, q=Q)
    ov = out.rearrange("b (k tq q) d -> k b tq (q d)", tq=STEPS // Q, q=Q)

    with ExitStack() as ctx:
        def sb(name, shape, dt=fp32):
            return ctx.enter_context(nc.sbuf_tensor(name, shape, dt))

        def pb(name, shape=(P, TOK)):
            return ctx.enter_context(nc.psum_tensor(name, list(shape), fp32))

        def sem(name):
            return ctx.enter_context(nc.semaphore(name))

        ident = sb("ident", [P, P])
        neghalf = sb("neghalf", [P, Q])
        scratch = sb("scratch", [P, 1])
        eps1, eps4 = sb("eps1", [P, Q]), sb("eps4", [P, Q])
        primer = sb("primer", [P, Q])
        napier = sb("napier", [P, Q, E])
        ws_t, wi_t, wsi_t = sb("ws_t", [N, D]), sb("wi_t", [N, D]), sb("wsi_t", [N, D])
        wo_t = sb("wo_t", [D, N])
        vrow, vcol = sb("vrow", [32, P]), sb("vcol", [P, 32])
        brow, bcol = sb("brow", [32, P]), sb("bcol", [P, 32])
        wg_t, gw_t, a_t = sb("wg_t", [D, D]), sb("gw_t", [E, D]), sb("a_t", [N, N])
        wsiT, woT, wgT, aT = sb("wsiT", [D, N]), sb("woT", [N + 1, D]), sb("wgT", [D, D]), sb("aT", [P, N])
        gwT2 = sb("gwT2", [D, 2 * E], fp32r)
        bu, bgh = sb("bu", [N, 1]), sb("bgh", [D, 1])
        gb = sb("gb", [P, E])
        w1f, w3f = sb("w1f", [D, HID + M13]), sb("w3f", [D, HID])
        w1h, w1l = sb("w1h", [D, HID + M13], fp32r), sb("w1l", [D, HID + M13], fp32r)
        w3h, w3l = sb("w3h", [D, HID], fp32r), sb("w3l", [D, HID], fp32r)
        b1c, b3c = bcol[:, 0:POS], bcol[:, POS:2 * POS]
        bgc, lnw, lnb = (vcol[:, i:i + 1] for i in range(3))
        bsc, bic = vcol[0:N, 3:4], vcol[0:N, 4:5]
        w2t = sb("w2t", [P, POS, D])
        w2h, w2l = sb("w2h", [P, POS, D], fp32r), sb("w2l", [P, POS, D], fp32r)
        self_, sel = sb("self_", [P, CH * P]), sb("sel", [P, CH * P], fp32r)

        xt = [sb(f"xt{i}", [P, Q, D]) for i in range(2)]
        xn = sb("xn", [P, Q, D])
        xnT = sb("xnT", [D, TOK])
        gth = [sb(f"gth{i}", [D, TOK]) for i in range(2)]
        hT = [sb(f"hT{i}", [P, TOK]) for i in range(2)]
        og = sb("og", [D, TOK])
        x1 = sb("x1", [P, Q, D])
        x1kept = [sb(f"x1kept{i}", [P, Q, D]) for i in range(2)]
        x1h = [sb(f"x1h{i}", [D, TOK], fp32r) for i in range(2)]
        x1l = [sb(f"x1l{i}", [D, TOK], fp32r) for i in range(2)]
        rwT = sb("rwT", [P, TOK], fp32r)
        rt = sb("rt", [P, Q, P])
        t3, zt = [sb(f"t3_{i}", [P, TOK]) for i in range(2)], [sb(f"zt{i}", [P, TOK]) for i in range(2)]
        sl = [sb(f"sl{i}", [P, TOK]) for i in range(2)]
        full = {w: sb(f"full_{w}", [P, TOK]) for w in ("sh0", "sh1", *range(FULLS))}
        high = {w: sb(f"high_{w}", [P, TOK], fp32r) for w in ("sh0", "sh1", *range(PARTS))}
        low = {w: sb(f"low_{w}", [P, TOK], fp32r) for w in ("sh0", "sh1", *range(PARTS))}
        yT = sb("yT", [D, TOK])
        yo = sb("yo", [P, Q, D])
        stats = {w: sb(f"stats_{w}", [P, Q, 6]) for w in ("in", "mid", "out")}
        mv = {w: sb(f"mv_{w}", [P, Q, 2]) for w in ("in", "mid", "out")}
        ve = {w: sb(f"ve_{w}", [P, Q]) for w in ("in", "mid", "out")}
        rstd = {w: sb(f"rstd_{w}", [P, Q]) for w in ("in", "mid", "out")}
        row = {w: sb(f"row_{w}", [P, Q]) for w in ("max", "sum", "inv")}
        ex8 = {w: sb(f"ex8_{w}", [P, Q, E]) for w in
               ("lg", "ls", "ex", "sc", "rw")}
        bz, taken = sb("bz", [P, Q, 2 * E]), sb("taken", [P, Q, 2 * E])
        top, best = sb("top", [P, Q, 8]), sb("best", [P, Q, 8])
        rwh = sb("rwh", [P, Q, E], fp32r)

        p1 = [pb(f"p1_{i}") for i in range(2)]
        p3 = [pb(f"p3_{i}") for i in range(2)]
        prw, py, pu, pm = pb("prw"), pb("py"), pb("pu"), pb("pm")

        vectors_loaded, biases_loaded, rows_zeroed = sem("vectors_loaded"), sem("biases_loaded"), sem("rows_zeroed")
        state_weights_loaded, out_weights_loaded = sem("state_weights_loaded"), sem("out_weights_loaded")
        up_weights_loaded, w2_loaded, gate_b_loaded = sem("up_weights_loaded"), sem("w2_loaded"), sem("gate_b_loaded")
        id_made, const_made, pool_step, sel_made = sem("id_made"), sem("const_made"), sem("pool_step"), sem("sel_made")
        w2_zeroed, setup_dve, setup_tr = sem("w2_zeroed"), sem("setup_dve"), sem("setup_tr")
        state_weights_ready, out_weights_ready = sem("state_weights_ready"), sem("out_weights_ready")
        expert_weights_ready, sel_ready = sem("expert_weights_ready"), sem("sel_ready")
        x_loaded = [sem("x_loaded0"), sem("x_loaded1")]
        out_stored = sem("out_stored")
        bn_done = {w: sem(f"bn_done_{w}") for w in ("in", "mid", "out")}
        mv_ready = {w: sem(f"mv_ready_{w}") for w in ("in", "mid", "out")}
        pool_r = {w: sem(f"pool_r_{w}") for w in ("in", "mid", "out")}
        xn_ready, xnT_ps, xnT_ready = sem("xn_ready"), sem("xnT_ps"), sem("xnT_ready")
        gate_ps, gate_ready = sem("gate_ps"), sem("gate_ready")
        h_ps, h_ready = sem("h_ps"), sem("h_ready")
        ho_ps, og_ready, ogT_ps, v_ready = sem("ho_ps"), sem("og_ready"), sem("ogT_ps"), sem("v_ready")
        x1_ready, x1T_ps, x1h_ready, x1l_ready = sem("x1_ready"), sem("x1T_ps"), sem("x1h_ready"), sem("x1l_ready")
        lg_ps, ls_ready, ex_ready, soft_step = sem("lg_ps"), sem("ls_ready"), sem("ex_ready"), sem("soft_step")
        rt_ready, rwT_ps, rwT_ready = sem("rt_ready"), sem("rwT_ps"), sem("rwT_ready")
        up_ps, t3_ready, z_ready, sl_ready = sem("up_ps"), sem("t3_ready"), sem("z_ready"), sem("sl_ready")
        rwb_ps, s_ready, down_ps = sem("rwb_ps"), sem("s_ready"), sem("down_ps")
        high_ready, low_ready = sem("high_ready"), sem("low_ready")
        yT_ready, y_ps, v2_ready, yo_ready = sem("yT_ready"), sem("y_ps"), sem("v2_ready"), sem("yo_ready")

        block = ctx.enter_context(nc.Block())

        def wait(eng, s, v):
            if not (isinstance(v, int) and v <= 0):
                eng.wait_ge(s, v)

        def iterations(eng, one):
            def straight(k):
                one(k, k % 2, k // 2, 0 <= k < TILES, 0 <= k + 1 < TILES, 0 <= k + 2 < TILES, k + 3 < TILES, 0 <= k - 1)
            for k in range(-3, 3):
                straight(k)
            with eng.Fori(0, (TILES - 6) // 2) as j:
                one(2 * j + 3, 1, j + 1, True, True, True, True, True)
                one(2 * j + 4, 0, j + 2, True, True, True, True, True)
            for k in range(TILES - 3, TILES + 1):
                straight(k)

        def cols(pos):
            if pos == 0:
                return slice(CH * P, HID)
            if pos == 1:
                return slice(HID, HID + M13)
            return slice((pos - 2) * P, (pos - 1) * P)

        def full_of(pos):
            return full[("sh0", "sh1")[pos]] if pos < 2 else full[pos % FULLS]

        def parts_of(pos):
            w = ("sh0", "sh1")[pos] if pos < 2 else pos % PARTS
            return high[w], low[w]

        def used(pos, k, turns):
            if pos < 2:
                return POS * (k - 1) + pos + 1
            if pos < 2 + turns:
                return POS * (k - 1) + max(p for p in range(2, POS) if p % turns == pos % turns) + 1
            return POS * k + pos - turns + 1

        def at(what, k):
            return AT_START[what] if isinstance(k, int) and k < 0 else AT[what]

        def out_bank(k):
            return py if isinstance(k, int) and k < 0 else pu

        def early(slot, k, norm, what):
            if isinstance(k, int) and k == -2 and slot == AT_START["second_" + what]:
                return k + 3
            return k + 2 if norm and slot == at(what, k) and not (isinstance(k, int) and k == -1) else None

        def transposed(slot, k, norm):
            return early(slot, k, norm, "xnT")

        def gated(slot, k, norm):
            return early(slot, k, norm, "gate")

        def chain_step(slot, k):
            first = isinstance(k, int) and k < 0
            slots = [at('chain', k) + (t if first else t * 9 // 5) for t in range(STEPS)]
            return slots.index(slot) if slot in slots else None

        def step_cols(t):
            tq, q = divmod(t, Q)
            return slice(q * P + tq, (q + 1) * P, STEPS // Q)

        @block.sync
        def _(sp):
            def row(v):
                return v.rearrange("(a d) -> a d", a=1)

            sp.dma_start(xt[0][:, :, :].rearrange("p q d -> p (q d)"), xv[0]).then_inc(x_loaded[0], 16)
            for dst, src in ((ws_t, Ws), (wi_t, Wi), (a_t, A), (wg_t, Wg)):
                sp.dma_start(dst[:, :], src).then_inc(state_weights_loaded, 16)
            sp.dma_start(xt[1][:, :, :].rearrange("p q d -> p (q d)"), xv[1]).then_inc(x_loaded[1], 16)
            for dst, src in ((wo_t[:, :], Wo), (gw_t[:, :], gate_w), (woT[N:N + 1, :], row(bo))):
                sp.dma_start(dst, src).then_inc(out_weights_loaded, 16)
            sp.dma_start(w1f[:, 0:CH * P].rearrange("d (e h) -> d e h", e=E), w1.rearrange("e d h -> d e h")).then_inc(up_weights_loaded, 16)
            sp.dma_start(w1f[:, CH * P:HID + REST], sw1).then_inc(up_weights_loaded, 16)
            sp.dma_start(w3f[:, CH * P:HID], sw3[:, 0:P]).then_inc(up_weights_loaded, 16)
            sp.dma_start(w1f[:, HID + 64:HID + M13], sw3[:, P:H]).then_inc(up_weights_loaded, 16)
            sp.wait_ge(rows_zeroed, 1)
            for r, at, src, ssrc in ((0, 0, b1, sb1), (POS, 64, b3, sb3)):
                sp.dma_start(brow[r + 2:r + POS, :], src.rearrange("e h -> (e h)").rearrange("(c p) -> c p", p=P)).then_inc(biases_loaded, 16)
                sp.dma_start(brow[r:r + 1, :], row(ssrc[0:P])).then_inc(biases_loaded, 16)
                sp.dma_start(brow[r + 1:r + 2, at:at + REST], row(ssrc[P:H])).then_inc(biases_loaded, 16)
            sp.dma_start(gb[:, :], gate_b.partition_broadcast(P)).then_inc(gate_b_loaded, 16)
            sp.dma_start(w2t[:, 2:POS, :], w2.rearrange("e h d -> (e h) d").rearrange("(c p) d -> p c d", p=P)).then_inc(w2_loaded, 16)
            sp.dma_start(w2t[:, 0, :], sw2[0:P, :]).then_inc(w2_loaded, 16)
            sp.wait_ge(w2_zeroed, 1)
            sp.dma_start(w2t[0:REST, 1, :], sw2[P:H, :]).then_inc(w2_loaded, 16)
            for at in (64, 96):
                sp.dma_start(w2t[at:at + E, 1, :], b2).then_inc(w2_loaded, 16)
                sp.dma_start(w2t[at + E:at + E + 1, 1, :], row(sb2)).then_inc(w2_loaded, 16)

            def one(k, par, half, moe, attn, norm, pre, fin):
                if attn and (not isinstance(k, int) or k + 3 < TILES):
                    sp.wait_ge(v_ready, k + 2)
                    sp.dma_start(xt[1 - par][:, :, :].rearrange("p q d -> p (q d)"),
                                 xv[bass.ds(k + 3, 1)].rearrange("a b t f -> (a b) t f") if not isinstance(k, int) else xv[k + 3]
                                 ).then_inc(x_loaded[1 - par], 16)
                if fin:
                    sp.wait_ge(yo_ready, k)
                    sp.dma_start(ov[bass.ds(k - 1, 1)].rearrange("a b t f -> (a b) t f") if not isinstance(k, int) else ov[k - 1],
                                 yo[:, :, :].rearrange("p q d -> p (q d)")).then_inc(out_stored, 16)
            iterations(sp, one)
            sp.wait_ge(out_stored, 16 * TILES)

        @block.gpsimd
        def _(g):
            g.memset(ident[:, :], 0.0).then_inc(pool_step, 1)
            g.wait_ge(pool_step, 1)
            g.affine_select(out=ident[:, :], in_=ident[:, :], compare_op=ALU.not_equal, fill=1.0,
                            base=0, pattern=[[-1, P]], channel_multiplier=1).then_inc(id_made, 1)
            g.memset(neghalf[:, :], -0.5)
            g.memset(eps1[:, :], EPS)
            g.memset(eps4[:, :], 4 * EPS)
            g.memset(napier[:, :, :], NAPIER)
            g.memset(bz[:, :, E:2 * E], FILLER)
            g.memset(best[:, :, 2:8], FILLER)
            g.memset(rt[:, :, :], 0.0).then_inc(pool_step, 1)
            g.wait_ge(pool_step, 2)
            g.memset(rt[:, :, E:E + 1], 1.0)
            g.memset(rt[:, :, 64 + E:65 + E], 1.0).then_inc(const_made, 1)

            def selector():
                g.wait_ge(pool_r["in"], 4)
                n = 0
                for r in (slice(0, P), slice(32, 64)):
                    v = self_[r, :]
                    g.memset(v, 1.0).then_inc(sel_made, 1)
                    n += 1
                    for base, step, height in ((0, 1, -H), (H - 1, -1, H)):
                        g.wait_ge(sel_made, n)
                        n += 1
                        g.affine_select(out=v, in_=v, compare_op=ALU.is_ge, fill=0.0, base=base,
                                        pattern=[[step, CH * P]], channel_multiplier=height).then_inc(sel_made, 1)
                    g.wait_ge(sel_made, n)

            def rsqrt(w, tile, eps_t):
                g.wait_ge(mv_ready[w], tile + 1)
                g.tensor_tensor(out=ve[w][:, :], in0=mv[w][:, :, 1], in1=eps_t[:, :], op=ALU.add).then_inc(pool_r[w], 1)
                g.wait_ge(pool_r[w], 2 * tile + 1)
                g.tensor_tensor(out=rstd[w][:, :], in0=ve[w][:, :], in1=neghalf[:, :], op=ALU.pow).then_inc(pool_r[w], 1)

            def low_part(pos, k):
                R = REST if pos == 1 else P
                hi, lo = parts_of(pos)
                g.wait_ge(high_ready, POS * k + pos + 1)
                g.tensor_tensor(out=lo[0:R, :], in0=full_of(pos)[0:R, :], in1=hi[0:R, :].bitcast(fp32),
                                op=ALU.subtract).then_inc(low_ready, 1)

            def one(k, par, half, moe, attn, norm, pre, fin):
                for pos in range(POS):
                    if pos == AT_POOL['mid'] and attn:
                        rsqrt("mid", k + 1, eps4)
                    if pos == AT_POOL['out'] and fin:
                        rsqrt("out", k - 1, eps1)
                    if pos == AT_POOL['fresh'] and pre:
                        rsqrt("in", k + 3, eps1)
                    if AT_POOL['exp'] <= pos < AT_POOL['exp'] + Q and attn:
                        g.wait_ge(ls_ready, k + 2)
                        q = pos - AT_POOL['exp']
                        g.tensor_tensor(out=ex8["ex"][:, q, :], in0=napier[:, q, :], in1=ex8["ls"][:, q, :],
                                        op=ALU.pow).then_inc(ex_ready, 1)
                    if moe and pos >= 2:
                        low_part(pos - 2, k)
                    elif fin and pos < 2:
                        low_part(POS - 2 + pos, k - 1)
                if isinstance(k, int) and k == -2:
                    selector()
            iterations(g, one)

        @block.scalar
        def _(act):
            act.wait_ge(rows_zeroed, 1)
            for r, src in enumerate((bg, ln_w, ln_b, bs, bi)):
                act.dma_start(vrow[r:r + 1, 0:src.shape[0]], src.rearrange("(a d) -> a d", a=1)).then_inc(vectors_loaded, 16)
            act.dma_start(w3f[:, 0:CH * P].rearrange("d (e h) -> d e h", e=E), w3.rearrange("e d h -> d e h")).then_inc(up_weights_loaded, 16)
            act.wait_ge(const_made, 1)
            nc.scalar.activation(primer[:, :], neghalf[:, :], ACT.Silu)

            def side(slot, k, par, half, moe, attn, norm, pre, fin):
                t = chain_step(slot, k)
                if norm and t is not None:
                    c = step_cols(t)
                    act.wait_ge(h_ps, STEPS * (k + 2) + t + 1)
                    nc.scalar.activation(hT[par][0:N, c], pu[0:N, c], ACT.Tanh, bias=bu[:, 0:1]).then_inc(h_ready, 1)
                if slot == AT['rwT'] and moe:
                    act.wait_ge(rwT_ps, k + 1)
                    nc.scalar.activation(rwT[:, :], pm[:, :], ACT.Identity)
                    nc.scalar.activation(high["sh1"][64:P, :], pm[64:P, :], ACT.Identity).then_inc(rwT_ready, 1)
                if slot == AT['yT'] and fin:
                    act.wait_ge(down_ps, POS * k)
                    wait(act, y_ps, k - 1)
                    nc.scalar.activation(yT[:, :], py[:, :], ACT.Identity).then_inc(yT_ready, 1)
                tile = transposed(slot, k, norm)
                if tile is not None:
                    act.wait_ge(xnT_ps, tile + 1)
                    nc.scalar.activation(xnT[:, :], pm[:, :], ACT.Identity, scale=lnw,
                                         bias=lnb).then_inc(xnT_ready, 1)
                tile = gated(slot, k, norm)
                if tile is not None:
                    act.wait_ge(gate_ps, tile + 1)
                    wait(act, og_ready, tile - 1)
                    gate_buffer = par if not (isinstance(k, int) and tile == k + 3) else 1 - par
                    nc.scalar.activation(gth[gate_buffer][:, :], pm[:, :], ACT.Tanh, scale=0.5,
                                         bias=bgh[:, 0:1]).then_inc(gate_ready, 1)
                if slot == at('x1T', k) + 1 and attn:
                    act.wait_ge(x1T_ps, k + 2)
                    nc.scalar.activation(x1h[1 - par][:, :], pm[:, :], ACT.Identity).then_inc(x1h_ready, 1)

            def silu(pos, par, k):
                act.wait_ge(z_ready, POS * k + pos + 1)
                if pos < 2:
                    R = REST if pos == 1 else P
                    wait(act, low_ready, POS * (k - 1) + pos + 1)
                    nc.scalar.activation(full_of(pos)[0:R, :], zt[(par + pos) % 2][0:R, :], ACT.Silu).then_inc(sl_ready, 1)
                else:
                    wait(act, s_ready, CH * k + max(pos - 3, 0))
                    nc.scalar.activation(sl[pos % 2][:, :], zt[(par + pos) % 2][:, :], ACT.Silu).then_inc(sl_ready, 1)

            def high_part(pos, k):
                R = REST if pos == 1 else P
                if pos < 2:
                    act.wait_ge(sl_ready, POS * k + pos + 1)
                else:
                    act.wait_ge(s_ready, CH * k + pos - 1)
                wait(act, down_ps, used(pos, k, PARTS))
                nc.scalar.activation(parts_of(pos)[0][0:R, :], full_of(pos)[0:R, :], ACT.Identity).then_inc(high_ready, 1)

            def one(k, par, half, moe, attn, norm, pre, fin):
                for pos in range(POS):
                    side(3 * pos, k, par, half, moe, attn, norm, pre, fin)
                    if moe:
                        act.wait_ge(up_ps, POS * k + pos + 1)
                        if pos == 1:
                            nc.scalar.activation(t3[par ^ 1][0:REST, :], p1[par ^ 1][64:M13, :], ACT.Identity,
                                                 bias=b3c[64:M13, 1:2]).then_inc(t3_ready, 1)
                        else:
                            nc.scalar.activation(t3[(par + pos) % 2][:, :], p3[(par + pos) % 2][:, :], ACT.Identity,
                                                 bias=b3c[:, pos:pos + 1]).then_inc(t3_ready, 1)
                    side(3 * pos + 1, k, par, half, moe, attn, norm, pre, fin)
                    if moe and pos >= 1:
                        silu(pos - 1, par, k)
                    elif fin and pos == 0:
                        silu(POS - 1, 1 - par, k - 1)
                    side(3 * pos + 2, k, par, half, moe, attn, norm, pre, fin)
                    if moe and pos >= 2:
                        high_part(pos - 2, k)
                    elif fin and pos < 2:
                        high_part(POS - 2 + pos, k - 1)
            act.wait_ge(state_weights_ready, 1)
            iterations(act, one)

        @block.vector
        def _(v):
            n = [0]

            def link(ins):
                n[0] += 1
                ins.then_inc(setup_dve, 1)
                v.wait_ge(setup_dve, n[0])

            nc.vector.memset(vrow[:, :], 0.0)
            nc.vector.memset(brow[:, :], 0.0).then_inc(rows_zeroed, 1)
            nc.vector.memset(aT[:, :], 0.0)
            nc.vector.memset(w2t[:, 1, :], 0.0).then_inc(w2_zeroed, 1)
            nc.vector.memset(w1f[:, HID + REST:HID + 64], 0.0)
            nc.vector.memset(hT[0][:, :], 1.0)
            link(nc.vector.memset(hT[1][:, :], 1.0))
            link(nc.vector.memset(hT[1][0:N, step_cols(STEPS - 1)], 0.0))

            def add_state_weights():
                v.wait_ge(state_weights_loaded, 16 * 4)
                link(nc.vector.tensor_tensor(out=wsi_t[:, :], in0=ws_t[:, :], in1=wi_t[:, :], op=ALU.add))

            def state_weights():
                v.wait_ge(setup_tr, 1)
                t = p1[0]
                link(nc.vector.tensor_copy(vcol[:, :], t[:, 320:352]))
                nc.vector.tensor_tensor(out=bu[:, :], in0=bsc, in1=bic, op=ALU.add)
                nc.vector.tensor_scalar(out=bgh[:, :], in0=bgc, scalar1=0.5, scalar2=None, op0=ALU.mult)
                nc.vector.tensor_copy(wsiT[:, 0:N], t[:, 0:N])
                nc.vector.tensor_copy(wgT[:, :], t[:, 144:144 + D])
                nc.vector.tensor_copy(aT[0:N, :], t[0:N, 272:272 + N]).then_inc(state_weights_ready, 1)

            def out_weights():
                v.wait_ge(setup_tr, 2)
                t = p1[1]
                nc.vector.memset(high["sh1"][:, :].bitcast(fp32), 0.0)
                nc.vector.memset(low["sh1"][:, :].bitcast(fp32), 0.0)
                nc.vector.tensor_copy(woT[0:N, :], t[0:N, 16:16 + D])
                link(nc.vector.tensor_copy(gwT2[:, 0:E], t[:, 288:288 + E]))
                nc.vector.tensor_tensor(out=gwT2[:, E:2 * E], in0=t[:, 288:288 + E], in1=gwT2[:, 0:E].bitcast(fp32),
                                        op=ALU.subtract).then_inc(out_weights_ready, 1)

            def expert_weights():
                v.wait_ge(up_weights_loaded, 16 * 5)
                nc.vector.tensor_copy(w1h[:, :], w1f[:, :])
                link(nc.vector.tensor_copy(w3h[:, :], w3f[:, :]))
                nc.vector.tensor_tensor(out=w1l[:, :], in0=w1f[:, :], in1=w1h[:, :].bitcast(fp32), op=ALU.subtract)
                nc.vector.tensor_tensor(out=w3l[:, :], in0=w3f[:, :], in1=w3h[:, :].bitcast(fp32), op=ALU.subtract)
                v.wait_ge(w2_loaded, 16 * 7)
                link(nc.vector.tensor_copy(w2h[:, :, :], w2t[:, :, :]))
                nc.vector.tensor_tensor(out=w2l[:, :, :], in0=w2t[:, :, :], in1=w2h[:, :, :].bitcast(fp32), op=ALU.subtract)
                v.wait_ge(setup_tr, 3)
                nc.vector.tensor_copy(bcol[:, :], p3[1][:, 0:32]).then_inc(expert_weights_ready, 1)

            def selector():
                v.wait_ge(sel_made, 6)
                nc.vector.tensor_copy(sel[:, :], self_[:, :]).then_inc(sel_ready, 1)

            def moments(w, src, tile):
                for q in range(Q):
                    ins = nc.vector.bn_stats(out=stats[w][:, q, :], in_=src[:, q, :])
                ins.then_inc(bn_done[w], 1)
                v.wait_ge(bn_done[w], tile + 1)
                nc.vector.memset(scratch[:, :], 0.0)
                for q in range(Q):
                    ins = nc.vector.bn_aggr(out=mv[w][:, q, :], in_=stats[w][:, q, :])
                ins.then_inc(mv_ready[w], 1)

            def normalize(w, src, dst, tile, ready):
                v.wait_ge(pool_r[w], 2 * tile + 2)
                for q in range(Q):
                    ins = nc.vector.tensor_scalar(out=dst[:, q, :], in0=src[:, q, :], scalar1=mv[w][:, q, 0:1],
                                                  scalar2=rstd[w][:, q:q + 1], op0=ALU.subtract, op1=ALU.mult)
                ins.then_inc(ready, 1)

            def bc(t):
                return t[:, :].unsqueeze(2).to_broadcast([P, Q, E])

            def router(step, tile):
                r, e8 = row, ex8
                lg = e8["lg"][:, :, :]
                gbb = gb[:, :].unsqueeze(1).to_broadcast([P, Q, E])
                tt = nc.vector.tensor_tensor

                if step == 0:
                    v.wait_ge(lg_ps, tile + 1)
                    ins = nc.vector.tensor_reduce(out=lg, in_=pm[:, 0:2 * Q * E].rearrange("p (q s e) -> p q e s", q=Q, s=2),
                                                  op=ALU.add, axis=AX.X)
                else:
                    v.wait_ge(soft_step, SOFT * tile + step)
                if step == 1:
                    ins = nc.vector.tensor_reduce(out=r["max"][:, :], in_=lg, op=ALU.max, axis=AX.X)
                if step == 2:
                    ins = tt(out=e8["ls"][:, :, :], in0=lg, in1=bc(r["max"]), op=ALU.subtract)
                    ins.then_inc(ls_ready, 1)
                    ins = nc.vector.memset(scratch[:, :], 0.0)
                if step == 3:
                    v.wait_ge(ex_ready, Q * (tile + 1))
                    ins = nc.vector.tensor_reduce(out=r["sum"][:, :], in_=e8["ex"][:, :, :], op=ALU.add, axis=AX.X)
                if step == 4:
                    ins = nc.vector.reciprocal(r["inv"][:, :], r["sum"][:, :])
                if step == 5:
                    ins = tt(out=e8["sc"][:, :, :], in0=e8["ex"][:, :, :], in1=bc(r["inv"]), op=ALU.mult)
                if step == 6:
                    if isinstance(tile, int) and tile == 0:
                        v.wait_ge(gate_b_loaded, 16)
                    ins = tt(out=bz[:, :, 0:E], in0=e8["sc"][:, :, :], in1=gbb, op=ALU.add)
                if step == 7:
                    nc.vector.memset(scratch[:, :], 0.0)
                    for q in range(Q):
                        ins = nc.vector.max(out=top[:, q, :], in_=bz[:, q, 0:E])
                if step == 8:
                    ins = nc.vector.tensor_copy(best[:, :, 0:2], top[:, :, 0:2])
                if step == 9:
                    nc.vector.memset(scratch[:, :], 0.0)
                    for q in range(Q):
                        ins = nc.vector.match_replace(out=taken[:, q, :], in_to_replace=best[:, q, :],
                                                      in_values=bz[:, q, :], imm_value=TAKEN)
                if step == 10:
                    for dst in (e8["rw"], rwh):
                        ins = nc.vector.scalar_tensor_tensor(out=dst[:, :, :], in0=taken[:, :, 0:E], scalar=TAKEN,
                                                             in1=e8["sc"][:, :, :], op0=ALU.is_equal, op1=ALU.mult)
                if step < SOFT:
                    ins.then_inc(soft_step, 1)
                else:
                    wait(v, rwT_ps, tile)
                    for at in (0, 64):
                        nc.vector.tensor_copy(rt[:, :, at:at + E], rwh[:, :, :].bitcast(fp32))
                        last = tt(out=rt[:, :, at + 32:at + 32 + E], in0=e8["rw"][:, :, :],
                                  in1=rwh[:, :, :].bitcast(fp32), op=ALU.subtract)
                    last.then_inc(rt_ready, 1)

            def side(slot, k, par, half, moe, attn, norm, pre, fin):
                if moe and 0 <= slot - AT['router_end'] < 5:
                    for step in range(3, SOFT + 1)[2 * (slot - AT['router_end']):2 * (slot - AT['router_end']) + 2]:
                        router(step, k)
                if slot == AT['og'] and attn:
                    v.wait_ge(ho_ps, k + 2)
                    v.wait_ge(gate_ready, k + 2)
                    nc.vector.scalar_tensor_tensor(out=og[:, :], in0=gth[1 - par][:, :], scalar=1.0, in1=out_bank(k)[:, :],
                                                   op0=ALU.add, op1=ALU.mult).then_inc(og_ready, 1)
                if slot == AT['x1'] and attn:
                    v.wait_ge(ogT_ps, k + 2)
                    nc.vector.scalar_tensor_tensor(out=x1[:, :, :], in0=xt[1 - par][:, :, :], scalar=4.0,
                                                   in1=out_bank(k)[:, :].rearrange("p (q d) -> p q d", q=Q),
                                                   op0=ALU.mult, op1=ALU.add).then_inc(v_ready, 1)
                    v.wait_ge(v_ready, k + 2)
                    moments("mid", x1, k + 1)
                if slot == AT['norm_mid'] and attn:
                    normalize("mid", x1, x1, k + 1, x1_ready)
                if slot == at('x1l', k) and attn:
                    v.wait_ge(x1h_ready, k + 2)
                    nc.vector.tensor_tensor(out=x1l[1 - par][:, :], in0=pm[:, :], in1=x1h[1 - par][:, :].bitcast(fp32),
                                            op=ALU.subtract).then_inc(x1l_ready, 1)
                if attn and 0 <= slot - at('router', k) < 3:
                    router(slot - at('router', k), k + 1)
                if slot == AT['v2'] and fin:
                    v.wait_ge(y_ps, k)
                    wait(v, out_stored, 16 * (k - 1))
                    nc.vector.tensor_tensor(out=yo[:, :, :], in0=pm[:, :].rearrange("p (q d) -> p q d", q=Q),
                                            in1=x1kept[1 - par][:, :, :], op=ALU.add).then_inc(v2_ready, 1)
                if slot == AT['moments_out'] and fin:
                    v.wait_ge(v2_ready, k)
                    moments("out", yo, k - 1)
                if slot == AT['kept'] and attn:
                    v.wait_ge(x1_ready, k + 2)
                    nc.vector.tensor_copy(x1kept[1 - par][:, :, :], x1[:, :, :])
                if slot == AT['moments_in'] and pre:
                    v.wait_ge(x_loaded[1 - par], 16 * (half + 2 + par))
                    moments("in", xt[1 - par], k + 3)
                if slot == AT['norm_out'] and fin:
                    normalize("out", yo, yo, k - 1, yo_ready)
                if slot == AT['norm_in'] and pre:
                    wait(v, xnT_ps, k + 3)
                    normalize("in", xt[1 - par], xn, k + 3, xn_ready)

            def weigh(pos, k):
                if pos < 2:
                    return
                v.wait_ge(sl_ready, POS * k + pos + 1)
                v.wait_ge(rwb_ps, CH * k + pos - 1)
                wait(v, low_ready, used(pos, k, FULLS))
                nc.vector.tensor_tensor(out=full_of(pos)[:, :], in0=prw[:, :], in1=sl[pos % 2][:, :],
                                        op=ALU.mult).then_inc(s_ready, 1)

            def one(k, par, half, moe, attn, norm, pre, fin):
                start = k if isinstance(k, int) else 0
                if start == -2:
                    state_weights()
                if start == -1:
                    expert_weights()
                for pos in range(POS):
                    side(3 * pos, k, par, half, moe, attn, norm, pre, fin)
                    if moe:
                        v.wait_ge(t3_ready, POS * k + pos + 1)
                        wait(v, sl_ready, POS * k + pos - 1)
                        R = REST if pos == 1 else P
                        nc.vector.scalar_tensor_tensor(out=zt[(par + pos) % 2][0:R, :], in0=p1[(par + pos) % 2][0:R, :],
                                                       scalar=b1c[0:R, pos:pos + 1], in1=t3[(par + pos) % 2][0:R, :],
                                                       op0=ALU.add, op1=ALU.mult).then_inc(z_ready, 1)
                    side(3 * pos + 1, k, par, half, moe, attn, norm, pre, fin)
                    side(3 * pos + 2, k, par, half, moe, attn, norm, pre, fin)
                    if moe and pos >= 1:
                        weigh(pos - 1, k)
                    elif fin and pos == 0:
                        weigh(POS - 1, k - 1)
                    if start == -1 and pos == 7:
                        selector()
                    if start == -3 and 3 * pos == 15:
                        add_state_weights()
                if start == -2:
                    out_weights()

            iterations(v, one)

        @block.tensor
        def _(pe):
            pe.wait_ge(id_made, 1)
            pe.wait_ge(setup_dve, 3)
            t = p1[0]
            nc.tensor.transpose(t[:, 0:N], wsi_t[:, :], ident[0:N, 0:N])
            nc.tensor.transpose(t[:, 144:144 + D], wg_t[:, :], ident[:, :])
            nc.tensor.transpose(t[0:N, 272:272 + N], a_t[:, :], ident[0:N, 0:N])
            pe.wait_ge(vectors_loaded, 16 * 5)
            nc.tensor.transpose(t[:, 320:352], vrow[:, :], ident[0:32, 0:32]).then_inc(setup_tr, 1)

            def out_weights():
                pe.wait_ge(out_weights_loaded, 16 * 3)
                nc.tensor.transpose(p1[1][0:N, 16:16 + D], wo_t[:, :], ident[:, :])
                nc.tensor.transpose(p1[1][:, 288:288 + E], gw_t[:, :], ident[0:E, 0:E]).then_inc(setup_tr, 1)

            def biases():
                pe.wait_ge(biases_loaded, 16 * 6)
                nc.tensor.transpose(p3[1][:, 0:32], brow[:, :], ident[0:32, 0:32]).then_inc(setup_tr, 1)

            def four_transposes(bank, src, s):
                for q in range(Q):
                    ins = nc.tensor.transpose(bank[:, q * P:(q + 1) * P], src(q), ident[:, :])
                ins.then_inc(s, 1)

            def side(slot, k, par, half, moe, attn, norm, pre, fin):
                tile = transposed(slot, k, norm)
                if tile is not None:
                    pe.wait_ge(xn_ready, tile + 1)
                    if isinstance(k, int) and k == -2:
                        wait(pe, gate_ready, tile)
                    else:
                        wait(pe, ls_ready, tile - 1)
                    four_transposes(pm, lambda q: xn[:, q, :], xnT_ps)
                if slot == AT['ho'] and attn:
                    pe.wait_ge(h_ready, STEPS * (k + 2))
                    nc.tensor.matmul(out_bank(k)[:, :], woT[:, :], hT[1 - par][0:N + 1, :], start=True, stop=True).then_inc(ho_ps, 1)
                tile = gated(slot, k, norm)
                if tile is not None:
                    pe.wait_ge(xnT_ready, tile + 1)
                    if isinstance(k, int) and tile == 0:
                        pe.wait_ge(state_weights_ready, 1)
                    nc.tensor.matmul(pm[:, :], wgT[:, :], xnT[:, :], start=True, stop=True).then_inc(gate_ps, 1)
                if slot == at('ogT', k) and attn:
                    pe.wait_ge(og_ready, k + 2)
                    four_transposes(out_bank(k), lambda q: og[:, q * P:(q + 1) * P], ogT_ps)
                if slot == AT['rwT'] and moe:
                    pe.wait_ge(rt_ready, k + 1)
                    if norm:
                        pe.wait_ge(gate_ready, k + 3)
                    else:
                        pe.wait_ge(v2_ready, k - 1)
                    four_transposes(pm, lambda q: rt[:, q, :], rwT_ps)
                if slot == at('u', k) and norm:
                    pe.wait_ge(xnT_ready, k + 3)
                    if moe:
                        pe.wait_ge(v_ready, k + 2)
                    nc.tensor.matmul(pu[0:N, :], wsiT[:, :], xnT[:, :], start=True, stop=True, skip_group_check=True)
                if isinstance(k, int) and k == -2 and slot == 3:
                    out_weights()
                if isinstance(k, int) and k == -1 and slot == 0:
                    biases()
                    pe.wait_ge(out_weights_ready, 1)
                t = chain_step(slot, k)
                if norm and t is not None:
                    c = step_cols(t)
                    before = hT[par if t else 1 - par][:, step_cols((t - 1) % STEPS)]
                    wait(pe, h_ready, STEPS * (k + 2) + t)
                    nc.tensor.matmul(pu[0:N, c], aT[:, :], before, start=False, stop=True,
                                     skip_group_check=True).then_inc(h_ps, 1)
                if slot == at('x1T', k) and attn:
                    pe.wait_ge(x1_ready, k + 2)
                    if moe:
                        pe.wait_ge(rwT_ready, k + 1)
                    elif norm:
                        pe.wait_ge(gate_ready, k + 3)
                    four_transposes(pm, lambda q: x1[:, q, :], x1T_ps)
                if slot == at('logits', k) and attn:
                    pe.wait_ge(x1l_ready, k + 2)
                    wait(pe, v2_ready, k)
                    for q in range(Q):
                        qs = slice(q * P, (q + 1) * P)
                        o = pm[:, 2 * q * E:2 * (q + 1) * E]
                        nc.tensor.matmul(o, x1h[1 - par][:, qs], gwT2[:, :], start=True, stop=False, skip_group_check=True)
                        ins = nc.tensor.matmul(o[:, 0:E], x1l[1 - par][:, qs], gwT2[:, 0:E], start=False, stop=True,
                                               skip_group_check=True)
                    ins.then_inc(lg_ps, 1)
                if slot == AT['yback'] and fin:
                    pe.wait_ge(yT_ready, k)
                    if attn:
                        pe.wait_ge(x1l_ready, k + 2)
                    elif moe:
                        pe.wait_ge(rwT_ready, k + 1)
                    else:
                        pe.wait_ge(v2_ready, k - 1)
                    four_transposes(pm, lambda q: yT[:, q * P:(q + 1) * P], y_ps)

            def broadcast(pos, k):
                if pos < 2:
                    return
                if pos == 2:
                    pe.wait_ge(rwT_ready, k + 1)
                wait(pe, s_ready, CH * k + pos - 2)
                nc.tensor.matmul(prw[:, :], sel[:, (pos - 2) * P:(pos - 1) * P], rwT[:, :],
                                 start=True, stop=True).then_inc(rwb_ps, 1)

            def split_product(o, wh, wl, par, done):
                nc.tensor.matmul(o, wl, x1h[par][:, :], start=True, stop=False)
                nc.tensor.matmul(o, wh, x1l[par][:, :], start=False, stop=False)
                ins = nc.tensor.matmul(o, wh, x1h[par][:, :], start=False, stop=True)
                if done is not None:
                    ins.then_inc(done, 1)

            def down(pos, k):
                if pos == 0:
                    wait(pe, yT_ready, k)
                pe.wait_ge(low_ready, POS * k + pos + 1)
                hi, lo = parts_of(pos)
                nc.tensor.matmul(py[:, :], w2h[:, pos, :], lo[:, :], start=(pos == 0), stop=False)
                nc.tensor.matmul(py[:, :], w2l[:, pos, :], hi[:, :], start=False, stop=False)
                nc.tensor.matmul(py[:, :], w2h[:, pos, :], hi[:, :], start=False,
                                 stop=(pos == POS - 1)).then_inc(down_ps, 1)

            def one(k, par, half, moe, attn, norm, pre, fin):
                start = k if isinstance(k, int) else 1
                if start == 0:
                    pe.wait_ge(expert_weights_ready, 1)
                for pos in range(POS):
                    if moe:
                        wait(pe, z_ready, POS * k + pos - 1)
                        bank = (par + pos) % 2
                        c = cols(pos)
                        o = p1[bank][0:c.stop - c.start, :]
                        split_product(o, w1h[:, c], w1l[:, c], par, up_ps if pos == 1 else None)
                    side(3 * pos, k, par, half, moe, attn, norm, pre, fin)
                    if moe and pos != 1:
                        split_product(p3[bank][:, :], w3h[:, c], w3l[:, c], par, up_ps)
                    side(3 * pos + 1, k, par, half, moe, attn, norm, pre, fin)
                    if start == 0 and pos == 3:
                        pe.wait_ge(sel_ready, 1)
                    if moe and pos >= LAG:
                        down(pos - LAG, k)
                    elif fin and pos < LAG:
                        down(POS - LAG + pos, k - 1)
                    if moe and pos >= 1:
                        broadcast(pos - 1, k)
                    elif fin and pos == 0:
                        broadcast(POS - 1, k - 1)
                    side(3 * pos + 2, k, par, half, moe, attn, norm, pre, fin)
            iterations(pe, one)


_INS = ["x", "Ws", "bs", "Wi", "bi", "Wo", "bo", "Wg", "bg", "ln_w", "ln_b", "A"]
_FFN = ["gate_w", "gate_b", "w1", "b1", "w3", "b3", "w2", "b2", "sw1", "sb1", "sw3", "sb3", "sw2", "sb2"]


def kernel(**inputs):
    import numpy as _np
    import concourse.bacc as _bacc
    from concourse import mybir as _mybir
    from concourse.bass_utils import run_bass_kernel_spmd as _run

    nc = _bacc.Bacc("TRN2", target_bir_lowering=False, num_devices=1)
    arrays, args = {}, []
    for name in [f"L0_attn_{n}" for n in _INS] + [f"L0_ffn_{n}" for n in _FFN]:
        a = _np.ascontiguousarray(inputs[name])
        arrays[f"in_{name}"] = a
        args.append(nc.dram_tensor(f"in_{name}", a.shape, _mybir.dt.from_np(a.dtype), kind="ExternalInput").ap())
    shape = arrays["in_L0_attn_x"].shape
    args.append(nc.dram_tensor("out", shape, _mybir.dt.float32, kind="ExternalOutput").ap())
    rnn_gate_moe_block(nc, *args)
    r = _run(nc, [arrays], core_ids=[0])
    return r.results[0]["out"]
```
